# Optimizing a Trainium2 kernel written in Bass

```python
import numpy as np
import jax
import jax.numpy as jnp

def _softmax(x, axis=-1):
    return jax.nn.softmax(x, axis=axis)

def _gelu(x):
    return jax.nn.gelu(x, approximate=True)

def _silu(x):
    return jax.nn.silu(x)

def _sigmoid(x):
    return jax.nn.sigmoid(x)

def _layernorm(x, axis=-1, eps=1e-05):
    m = jnp.mean(x, axis=axis, keepdims=True)
    v = jnp.var(x, axis=axis, keepdims=True)
    return (x - m) / jnp.sqrt(v + eps)

def _scatter_add(tgt, idx, src, axis=0):
    return tgt.at[idx].add(src)

def _segment_sum(src, seg, n):
    return jax.ops.segment_sum(src, seg, n)
kernel_name = 'mk_adj_resnorm_d2_adj_r2_0a1044'

def setup_inputs(seed: int=0):
    np.random.seed(seed)
    _w = jnp.asarray

    def _rec_inputs():
        import jax
        import jax.numpy as jnp
        _gk = jax.random.key(seed)
        x = -0.000125 + 0.9999 * jax.random.normal(jax.random.fold_in(_gk, 1), (128, 128, 128), jnp.float32)
        _w = (1.0 + jnp.arange(128, dtype=jnp.float32)) ** (-0.5)
        _w = _w / _w.mean()
        _pij = jnp.clip(0.03125 * _w[:, None] * _w[None, :], 0.0, 1.0)
        _a = jax.random.uniform(jax.random.fold_in(_gk, 2), (128, 128)) < _pij
        _a = jnp.logical_or(_a, jnp.swapaxes(_a, -1, -2))
        _a = jnp.logical_or(_a, jnp.eye(128, dtype=bool))
        _af = _a.astype(jnp.float32)
        _af = _af * jax.random.uniform(jax.random.fold_in(_gk, 3), (128, 128), jnp.float32, 0.05, 0.000488281)
        adj = _af
        return (x, adj)
    x, adj = _rec_inputs()

    def _L0_gnn_setup():
        import jax, jax.numpy as jnp
        import numpy as np
        B, T, D, H = (64, 1024, 128, 128)
        MAX_SKIP = 4

        def _lstm_last(Wih, Whh, bih, bhh, xs):
            N, _, Hd = xs.shape
            bias = bih + bhh

            def step(carry, x_t):
                h, c = carry
                g = x_t @ Wih.T + h @ Whh.T + bias
                i, f, gg, o = jnp.split(g, 4, axis=-1)
                c = jax.nn.sigmoid(f) * c + jax.nn.sigmoid(i) * jnp.tanh(gg)
                h = jax.nn.sigmoid(o) * jnp.tanh(c)
                return ((h, c), None)
            init = (jnp.zeros((N, Hd), xs.dtype), jnp.zeros((N, Hd), xs.dtype))
            (h_last, _), _ = jax.lax.scan(step, init, jnp.swapaxes(xs, 0, 1))
            return h_last
        key = jax.random.key(seed)
        ks = jax.random.split(key, 8)
        s = 0.05
        x = jax.random.normal(ks[0], (B, T, D), jnp.float32)
        adj = jax.random.uniform(ks[1], (T, T), jnp.float32) / T
        Wg0 = jax.random.normal(ks[2], (D, H), jnp.float32) * s
        bg0 = jnp.zeros((H,), jnp.float32)
        Wg1 = jax.random.normal(ks[3], (H, H), jnp.float32) * s
        bg1 = jnp.zeros((H,), jnp.float32)
        Wih = jax.random.normal(ks[4], (MAX_SKIP, 4 * H, H), jnp.float32) * s
        Whh = jax.random.normal(ks[5], (MAX_SKIP, 4 * H, H), jnp.float32) * s
        bih = jax.random.normal(ks[6], (MAX_SKIP, 4 * H), jnp.float32) * s
        bhh = jax.random.normal(ks[7], (MAX_SKIP, 4 * H), jnp.float32) * s
        return dict(x=x, adj=adj, Wg0=Wg0, bg0=bg0, Wg1=Wg1, bg1=bg1, Wih=Wih, Whh=Whh, bih=bih, bhh=bhh)
    _L0_gnn_all = _L0_gnn_setup()
    _L0_gnn_in = {k: v for k, v in _L0_gnn_all.items() if k in ('Wg0', 'bg0', 'Wg1', 'bg1', 'Wih', 'Whh', 'bih', 'bhh')}
    del _L0_gnn_all

    def _L1_gnn_setup():
        import jax, jax.numpy as jnp
        import numpy as np
        B, J, F_IN, F_OUT = (8192, 17, 128, 128)
        key = jax.random.key(seed)
        k1, k2, k3, k4 = jax.random.split(key, 4)
        gain = 1.414
        bound = gain * np.sqrt(6.0 / (F_IN + F_OUT))
        W = jax.random.uniform(k2, (3, F_IN, F_OUT), dtype=jnp.float32, minval=-bound, maxval=bound)
        stdv = 1.0 / np.sqrt(F_OUT)
        bias = jax.random.uniform(k4, (F_OUT,), dtype=jnp.float32, minval=-stdv, maxval=stdv)
        return {'x': jax.random.normal(k1, (B, J, F_IN), dtype=jnp.float32), 'W': W, 'adj': jax.random.uniform(k3, (J, J), dtype=jnp.float32), 'bias': bias}
    _L1_gnn_all = _L1_gnn_setup()
    _L1_gnn_in = {k: v for k, v in _L1_gnn_all.items() if k in ('W', 'bias')}
    del _L1_gnn_all
    return {'x': x, 'adj': adj, 'L0_gnn_Wg0': _L0_gnn_in['Wg0'], 'L0_gnn_bg0': _L0_gnn_in['bg0'], 'L0_gnn_Wg1': _L0_gnn_in['Wg1'], 'L0_gnn_bg1': _L0_gnn_in['bg1'], 'L0_gnn_Wih': _L0_gnn_in['Wih'], 'L0_gnn_Whh': _L0_gnn_in['Whh'], 'L0_gnn_bih': _L0_gnn_in['bih'], 'L0_gnn_bhh': _L0_gnn_in['bhh'], 'L1_gnn_W': _L1_gnn_in['W'], 'L1_gnn_bias': _L1_gnn_in['bias']}

def reference(x, adj, L0_gnn_Wg0, L0_gnn_bg0, L0_gnn_Wg1, L0_gnn_bg1, L0_gnn_Wih, L0_gnn_Whh, L0_gnn_bih, L0_gnn_bhh, L1_gnn_W, L1_gnn_bias):
    import jax
    import jax.numpy as jnp

    def _L0_gnn_ref(x, adj, Wg0, bg0, Wg1, bg1, Wih, Whh, bih, bhh):
        import jax, jax.numpy as jnp
        import numpy as np
        B, T, D, H = (64, 1024, 128, 128)
        MAX_SKIP = 4

        def _lstm_last(Wih, Whh, bih, bhh, xs):
            N, _, Hd = xs.shape
            bias = bih + bhh

            def step(carry, x_t):
                h, c = carry
                g = x_t @ Wih.T + h @ Whh.T + bias
                i, f, gg, o = jnp.split(g, 4, axis=-1)
                c = jax.nn.sigmoid(f) * c + jax.nn.sigmoid(i) * jnp.tanh(gg)
                h = jax.nn.sigmoid(o) * jnp.tanh(c)
                return ((h, c), None)
            init = (jnp.zeros((N, Hd), xs.dtype), jnp.zeros((N, Hd), xs.dtype))
            (h_last, _), _ = jax.lax.scan(step, init, jnp.swapaxes(xs, 0, 1))
            return h_last
        h = jax.nn.relu(jnp.einsum('ts,bsh->bth', adj, x @ Wg0 + bg0))
        h = jax.nn.relu(jnp.einsum('ts,bsh->bth', adj, h @ Wg1 + bg1))
        Bv, Tv, Hd = h.shape
        for p in range(1, MAX_SKIP + 1):
            nw = Tv // p
            wins = h[:, :nw * p, :].reshape(Bv * nw, p, Hd)
            last = _lstm_last(Wih[p - 1], Whh[p - 1], bih[p - 1], bhh[p - 1], wins)
            idx = jnp.arange(nw) * p + (p - 1)
            h = h.at[:, idx, :].set(last.reshape(Bv, nw, Hd))
        return h

    def _L1_gnn_ref(x, W, adj, bias):
        import jax, jax.numpy as jnp
        import numpy as np
        B, J, F_IN, F_OUT = (8192, 17, 128, 128)
        adj_0 = jnp.diag(jnp.diagonal(adj))
        adj_1 = jnp.triu(adj, k=1)
        adj_2 = jnp.tril(adj, k=-1)
        h = jnp.einsum('bjf,kfo->kbjo', x, W)
        out = jnp.einsum('ij,bjo->bio', adj_0, h[0]) + jnp.einsum('ij,bjo->bio', adj_1, h[1]) + jnp.einsum('ij,bjo->bio', adj_2, h[2])
        return out + bias[None, None, :]
    x = _layernorm(x + _L0_gnn_ref(x, adj, L0_gnn_Wg0, L0_gnn_bg0, L0_gnn_Wg1, L0_gnn_bg1, L0_gnn_Wih, L0_gnn_Whh, L0_gnn_bih, L0_gnn_bhh), axis=-1)
    x = _layernorm(x + _L1_gnn_ref(x, L1_gnn_W, adj, L1_gnn_bias), axis=-1)
    return x

_drawn_inputs = setup_inputs


def setup_inputs(seed=0):
    import zlib

    import numpy as np

    out = dict(_drawn_inputs(seed))
    spreads = {'L0_gnn_bg0': (0.0, 0.8), 'L0_gnn_bg1': (0.0, 0.8)}
    factors = {'L0_gnn_Wg0': 8.0,
     'L0_gnn_Wg1': 8.0,
     'L0_gnn_Wih': 8.0,
     'L0_gnn_Whh': 8.0,
     'L0_gnn_bih': 2.76,
     'L0_gnn_bhh': 2.811}
    for name, (base, spread) in spreads.items():
        noise = np.random.default_rng([zlib.crc32(name.encode()), seed]).standard_normal(out[name].shape)
        drawn = base * np.exp(spread * noise) if base else spread * noise
        out[name] = jnp.asarray(drawn.astype(out[name].dtype))
    for name, factor in factors.items():
        out[name] = (out[name] * factor).astype(out[name].dtype)
    return out
```

```python
import concourse.bass as bass
from concourse import mybir
from contextlib import ExitStack

B, T, D = 128, 128, 128
LEVELS = 4
CB = 16
CHUNKS = B // CB
CT = CB * T
STREAMS = 2
SB = CB // STREAMS
BANK = 512
WSCALE = 64.0
EPS = 1e-5
GI, GF, GG, GO = range(4)


def steps(p, s, stream):
    return [("L", p, s, stream, part) for part in range(SB * T // BANK if p == 1 else 1)]


def gate_list(stage):
    return (GG, GI, GO) if stage[2] == 0 else (GG, GI, GF, GO)


def body(gcn, post):
    def g(name):
        return [(name,)] if gcn else []

    def q(*name):
        return [name] if post else []

    def l(p, s, a):
        return steps(p, s, a)

    return (g("loadx") + q("T", 0) + l(1, 0, 0) + q("T", 1) + [("loadr",)] + l(1, 0, 1) + q("norm1")
            + g("gZ") + l(2, 0, 0) + g("gH1") + l(2, 0, 1) + l(2, 1, 0) + g("gY") + l(2, 1, 1) + g("gH2")
            + l(3, 0, 0) + q("K", 0) + l(3, 0, 1) + l(3, 1, 0) + q("K", 1) + l(3, 1, 1)
            + l(3, 2, 0) + q("K", 2) + l(3, 2, 1) + l(4, 0, 0) + q("K", 3) + l(4, 0, 1)
            + l(4, 1, 0) + q("O", 0) + l(4, 1, 1) + l(4, 2, 0) + q("O", 1) + l(4, 2, 1)
            + l(4, 3, 0) + q("norm2") + l(4, 3, 1))


PROLOGUE = [("loadx",), ("gZ",), ("gH1",), ("gY",), ("gH2",)]
EPILOGUE = [("T", 0), ("T", 1), ("norm1",), ("K", 0), ("K", 1), ("K", 2), ("K", 3), ("O", 0), ("O", 1),
            ("norm2",)]
NO_PSUM = ("loadx", "loadr", "norm1", "norm2")

ADDS = {
    "loadx": {"xg_loaded": 16},
    "loadr": {"xr_loaded": 16},
    "gZ": {"for_act": 1, "z_ready": 1},
    "gH1": {"for_dve": 1, "h1_ready": 1},
    "gY": {"for_dve": 1, "y_ready": 1},
    "gH2": {"for_act": 1, "h2_ready": 1},
    "T": {"for_dve": 1, "u_ready": 1},
    "K": {"for_act": 1, "zk_ready": 1},
    "O": {"for_dve": 1, "v_ready": 1},
    "norm1": {"var_ready": 1, "rstd_ready": 1, "xn_ready": 1, "r_ready": 1, "dve_order": 7},
    "norm2": {"var_ready": 1, "rstd_ready": 1, "out_ready": 1, "stored": 16, "dve_order": 7},
}
READ_BY = {"gZ": "z_ready", "gH1": "h1_ready", "gY": "y_ready", "gH2": "h2_ready", "T": "u_ready",
           "K": "zk_ready", "O": "v_ready", "L": "acts"}


def adds(stage):
    if stage[0] != "L":
        return ADDS[stage[0]]
    n = len(gate_list(stage))
    return {"gates": n, "acts": n, "c_ready": 1, "tanhc": 1, "h_done": 1, "dve_order": 4 if stage[2] else 2}


NAMES = sorted({n for a in ADDS.values() for n in a} | set(adds(("L", 1, 1, 0, 0))))


class Segment:

    def __init__(self, stages, turns, chunk, before):
        self.stages, self.turns, self.chunk = stages, turns, chunk
        self.start = before.end() if before else dict.fromkeys(NAMES, 0)
        self.before = before
        self.through = []
        now = dict(self.start)
        for stage in stages:
            for name, n in adds(stage).items():
                now[name] += n
            self.through.append(dict(now))
        self.per_turn = {n: now[n] - self.start[n] for n in NAMES}
        self.slots = [k for k, s in enumerate(stages) if s[0] not in NO_PSUM]
        assert len(self.slots) % 2 == 0

    def end(self):
        return {n: self.start[n] + self.turns * self.per_turn[n] for n in NAMES}

    def half(self, k):
        return self.slots.index(k) % 2


def make_segments():
    segs = [Segment(PROLOGUE, 1, 0, None)]
    segs.append(Segment(body(True, False), 1, 0, segs[-1]))
    segs.append(Segment(body(True, True), CHUNKS - 2, 1, segs[-1]))
    segs.append(Segment(body(False, True), 1, CHUNKS - 1, segs[-1]))
    segs.append(Segment(EPILOGUE, 1, CHUNKS, segs[-1]))
    return segs


def build(nc, x, adj_t, w_ih, w_hh, b_ih, b_hh, wg0, bg0, wg1, bg1, w_l1, b_l1, out):
    fp32, fp16 = mybir.dt.float32, mybir.dt.float16
    ALU, ACT = mybir.AluOpType, mybir.ActivationFunctionType
    segments = make_segments()
    ctx = ExitStack()
    with ctx:
        def sb(name, shape, dt=fp32):
            return ctx.enter_context(nc.sbuf_tensor(name, shape, dt))

        def sem(name):
            return ctx.enter_context(nc.semaphore(name))

        adj_sb = sb("adj_sb", [T, T])
        adj3 = sb("adj3", [T, 3, T])
        wg0_sb = sb("wg0_sb", [D, D])
        wg1_sb = sb("wg1_sb", [D, D])
        wl1_sb = sb("wl1_sb", [D, 3, D])
        wih_sb = sb("wih_sb", [D, LEVELS, 4, D])
        whh_sb = sb("whh_sb", [D, LEVELS - 1, 4, D])
        wih_hi = sb("wih_hi", [D, LEVELS - 1, 4, D], fp16)
        wih_lo = sb("wih_lo", [D, LEVELS - 1, 4, D], fp16)
        whh_hi = sb("whh_hi", [D, LEVELS - 1, 4, D], fp16)
        whh_lo = sb("whh_lo", [D, LEVELS - 1, 4, D], fp16)
        bih_sb = sb("bih_sb", [D, LEVELS, 4])
        bhh_sb = sb("bhh_sb", [D, LEVELS, 4])
        gate_bias = sb("gate_bias", [D, LEVELS, 4])
        bg0_rows = sb("bg0_rows", [T, D])
        bg1_rows = sb("bg1_rows", [T, D])
        bl1_rows = sb("bl1_rows", [T, D])
        bias1 = sb("bias1", [D, T])
        neg_bias1 = sb("neg_bias1", [D, T])
        bias2 = sb("bias2", [T, D])
        ident = sb("ident", [D, D], fp16)
        minus_half = sb("minus_half", [T, CB])
        xg = sb("xg", [T, CB, D])
        xr = sb("xr", [T, CB, D])
        z = sb("z", [D, CB, T])
        h1 = sb("h1", [D, CB, T])
        y = sb("y", [T, CB, D])
        h2 = sb("h2", [D, CB, T])
        h_hi = sb("h_hi", [D, CB, T], fp16)
        h_lo = sb("h_lo", [D, CB, T], fp16)
        u = sb("u", [T, CB, D])
        xn = sb("xn", [T, CB, D])
        r = sb("r", [T, CB, D])
        zk = sb("zk", [D, CB, 3, T])
        v = sb("v", [T, CB, D])
        stats = sb("stats", [T, CB, 6])
        mean = sb("mean", [T, CB])
        diff = sb("diff", [T, CB])
        var = sb("var", [T, CB])
        rstd = sb("rstd", [T, CB])
        gate = [[sb(f"gate{n}_{g}", [D, BANK]) for g in range(4)] for n in range(2)]
        tanh_c = [sb(f"tanh_c{n}", [D, BANK]) for n in range(2)]
        h_new = [sb(f"h_new{n}", [D, BANK]) for n in range(2)]
        cell = [sb(f"cell{a}", [D, BANK]) for a in range(STREAMS)]
        prev_hi = [sb(f"prev_hi{a}", [D, BANK], fp16) for a in range(STREAMS)]
        prev_lo = [sb(f"prev_lo{a}", [D, BANK], fp16) for a in range(STREAMS)]
        ps = ctx.enter_context(nc.psum_tensor("ps", [128, 2, 4, BANK], fp32))

        S = {name: sem(name) for name in NAMES}
        w_loaded = sem("w_loaded")
        more_loaded = sem("more_loaded")
        masks_made = sem("masks_made")
        split_done = sem("split_done")
        bias_ps = sem("bias_ps")
        bias_made = sem("bias_made")

        def value(seg, n, name, k=None):
            at = seg.start[name] if k is None else seg.through[k][name]
            return at if n is None else n * seg.per_turn[name] + at

        def find(seg, k, *stage):
            at = seg.stages.index(stage)
            assert at < k
            return at

        def walk(eng, run):
            for seg in segments:
                if seg.turns == 1:
                    for k, stage in enumerate(seg.stages):
                        run(seg, None, k, stage)
                else:
                    with eng.Fori(0, seg.turns) as n:
                        for k, stage in enumerate(seg.stages):
                            run(seg, n, k, stage)

        def lstm_index(seg, k):
            return sum(s[0] == "L" for s in seg.stages[:k])

        def windows(stage):
            return SB * (T // stage[1]) if stage[1] > 1 else BANK

        def positions(arr, stage):
            _, p, s, stream, part = stage
            if p == 1:
                b0 = stream * SB + part * (BANK // T)
                return arr[:, b0:b0 + BANK // T, :]
            n = T // p
            part_of = arr[:, stream * SB:(stream + 1) * SB, 0:n * p]
            return part_of.rearrange("h b (w s) -> h b w s", s=p)[:, :, :, s]

        def shaped(ap, stage):
            return ap[:, 0:windows(stage)].rearrange("h (b w) -> h b w", w=T // stage[1])

        block = ctx.enter_context(nc.Block())

        @block.sync
        def _(sp):
            for dst, src in ((adj_sb[:, :], adj_t), (wg0_sb[:, :], wg0), (bg0_rows[:, :], bg0),
                             (wg1_sb[:, :], wg1), (bg1_rows[:, :], bg1)):
                sp.dma_start(dst, src).then_inc(w_loaded, 16)

            def run(seg, n, k, stage):
                chunk = seg.chunk if n is None else n + seg.chunk
                if stage == ("loadx",):
                    ahead = 0 if seg is segments[0] else 1
                    if ahead:
                        sp.wait_ge(S["z_ready"], value(seg, n, "z_ready"))
                    sp.dma_start(xg[:, :, :], x[:, bass.ds((chunk + ahead) * CB, CB), :]
                                 ).then_inc(S["xg_loaded"], 16)
                elif stage == ("loadr",):
                    if seg.chunk:
                        sp.wait_ge(S["u_ready"], value(seg, n, "u_ready", k))
                    sp.dma_start(xr[:, :, :], x[:, bass.ds(chunk * CB, CB), :]).then_inc(S["xr_loaded"], 16)
                elif stage == ("norm2",):
                    sp.wait_ge(S["out_ready"], value(seg, n, "out_ready", k))
                    sp.dma_start(out[:, bass.ds((chunk - 1) * CB, CB), :], v[:, :, :]
                                 ).then_inc(S["stored"], 16)

            first = segments[0]
            run(first, None, 0, first.stages[0])
            for dst, src in ((wih_sb[:, :, :, :], w_ih), (bih_sb[:, :, :], b_ih), (bhh_sb[:, :, :], b_hh),
                             (whh_sb[:, :, :, :], w_hh), (wl1_sb[:, :, :], w_l1), (bl1_rows[:, :], b_l1)):
                sp.dma_start(dst, src).then_inc(more_loaded, 16)
            for seg in segments[1:]:
                if seg.turns == 1:
                    for k, stage in enumerate(seg.stages):
                        run(seg, None, k, stage)
                else:
                    with sp.Fori(0, seg.turns) as n:
                        for k, stage in enumerate(seg.stages):
                            run(seg, n, k, stage)
            sp.wait_ge(S["stored"], segments[-1].end()["stored"])

        FIRST_LOADS, MORE_LOADS = 5 * 16, 6 * 16

        @block.gpsimd
        def _(pool):
            nc.gpsimd.memset(ident[:, :], 0.0).then_inc(masks_made, 1)
            nc.gpsimd.memset(minus_half[:, :], -0.5).then_inc(masks_made, 1)
            pool.wait_ge(masks_made, 1)
            nc.gpsimd.affine_select(out=ident[:, :], in_=ident[:, :], compare_op=ALU.not_equal, fill=1.0,
                                    base=0, pattern=[[-1, D]], channel_multiplier=1).then_inc(masks_made, 1)
            pool.wait_ge(w_loaded, FIRST_LOADS)
            for part, (op, sign) in enumerate(((ALU.is_equal, 1), (ALU.is_gt, 1), (ALU.is_gt, -1))):
                nc.gpsimd.affine_select(out=adj3[:, part, :], in_=adj_sb[:, :], compare_op=op, fill=0.0,
                                        base=0, pattern=[[-sign, T]],
                                        channel_multiplier=sign).then_inc(masks_made, 1)

            pool.wait_ge(more_loaded, MORE_LOADS)

            def run(seg, n, k, stage):
                if stage in (("norm1",), ("norm2",)):
                    pool.wait_ge(S["var_ready"], value(seg, n, "var_ready", k))
                    nc.gpsimd.tensor_tensor(out=rstd[:, :], in0=var[:, :], in1=minus_half[:, :],
                                            op=ALU.pow).then_inc(S["rstd_ready"], 1)
                if stage == ("norm1",):
                    pool.wait_ge(S["xn_ready"], value(seg, n, "xn_ready", k))
                    nc.gpsimd.tensor_tensor(out=r[:, :, :], in0=xn[:, :, :],
                                            in1=bl1_rows[:, :].unsqueeze(1).broadcast_to([T, CB, D]),
                                            op=ALU.add).then_inc(S["r_ready"], 1)

            pool.wait_ge(masks_made, 6)
            walk(pool, run)

        @block.scalar
        def _(act):
            def run(seg, n, k, stage):
                kind = stage[0]
                if kind in ("gZ", "gH2", "K"):
                    act.wait_ge(S["for_act"], value(seg, n, "for_act", k))
                    half = seg.half(k)
                if kind == "gZ":
                    nc.scalar.activation(z[:, :, :], ps[:, half, :, :].rearrange("d q (b t) -> d (q b) t", t=T),
                                         ACT.Copy).then_inc(S["z_ready"], 1)
                elif kind == "gH2":
                    nc.scalar.activation(h2[:, :, :], ps[:, half, :, :].rearrange("d q (b t) -> d (q b) t", t=T),
                                         ACT.Relu).then_inc(S["h2_ready"], 1)
                elif kind == "K":
                    b0 = 4 * stage[1]
                    nc.scalar.activation(zk[:, b0:b0 + 4, :, :].rearrange("d b k t -> d b (k t)"),
                                         ps[:, half, :, 0:3 * T], ACT.Copy).then_inc(S["zk_ready"], 1)
                elif kind == "L":
                    _, p, s, stream, part = stage
                    unit, half, w = lstm_index(seg, k) % 2, seg.half(k), windows(stage)
                    gates = gate_list(stage)
                    before = value(seg, n, "h_done", k)
                    if not (seg.start["h_done"] == 0 and lstm_index(seg, k) < 2):
                        act.wait_ge(S["h_done"], before - 2)
                    ready = value(seg, n, "gates", k)
                    for j, g in enumerate(gates):
                        act.wait_ge(S["gates"], ready - len(gates) + 1 + j)
                        nc.scalar.activation(gate[unit][g][:, 0:w], ps[:, half, g, 0:w],
                                             ACT.Tanh if g == GG else ACT.Sigmoid,
                                             bias=gate_bias[:, p - 1, g:g + 1],
                                             scale=1.0 if p == 1 else 1.0 / WSCALE).then_inc(S["acts"], 1)
                    act.wait_ge(S["c_ready"], value(seg, n, "c_ready", k))
                    nc.scalar.activation(tanh_c[unit][:, 0:w], cell[stream][:, 0:w],
                                         ACT.Tanh).then_inc(S["tanhc"], 1)

            act.wait_ge(split_done, 6)
            walk(act, run)

        @block.vector
        def _(dve):
            dve.wait_ge(bias_ps, 1)
            nc.vector.tensor_copy(bias1[:, :], ps[:, 0, 0, 0:T]).then_inc(bias_made, 1)
            nc.vector.tensor_scalar(neg_bias1[:, :], ps[:, 0, 0, 0:T], -1.0, None, ALU.mult).then_inc(bias_made, 1)
            dve.wait_ge(bias_ps, 2)
            nc.vector.tensor_tensor(out=bias2[:, :], in0=ps[:, 1, 0, 0:D], in1=bg1_rows[:, :],
                                    op=ALU.add).then_inc(bias_made, 1)
            dve.wait_ge(bias_made, 3)
            dve.wait_ge(more_loaded, MORE_LOADS)
            nc.vector.tensor_tensor(out=gate_bias[:, :, :], in0=bih_sb[:, :, :], in1=bhh_sb[:, :, :],
                                    op=ALU.add).then_inc(split_done, 1)
            pairs = ((wih_sb[:, 1:LEVELS, :, :], wih_hi, wih_lo), (whh_sb[:, :, :, :], whh_hi, whh_lo))
            flat = "k p g n -> k (p g n)"
            for w, hi, lo in pairs:
                nc.vector.tensor_scalar(hi[:, :, :, :].rearrange(flat), w.rearrange(flat), WSCALE, None,
                                        ALU.mult).then_inc(split_done, 1)
            dve.wait_ge(split_done, 3)
            for w, hi, lo in pairs:
                nc.vector.scalar_tensor_tensor(out=lo[:, :, :, :].rearrange(flat), in0=w.rearrange(flat),
                                               scalar=WSCALE, in1=hi[:, :, :, :].rearrange(flat),
                                               op0=ALU.mult, op1=ALU.subtract).then_inc(split_done, 1)
            dve.wait_ge(split_done, 5)
            nc.vector.memset(mean[:, :], 0.0).then_inc(split_done, 1)
            dve.wait_ge(split_done, 6)

            def normalise(seg, n, k, src, dst, done):
                base = value(seg, n, "dve_order", k) - 7
                count = [0]

                def link(ins, wait=True):
                    count[0] += 1
                    ins.then_inc(S["dve_order"], 1)
                    if wait:
                        dve.wait_ge(S["dve_order"], base + count[0])

                for b in range(CB):
                    last = nc.vector.bn_stats(stats[:, b, :], src[:, b, :])
                link(last)
                even, odd = stats[:, :, 1], stats[:, :, 4]
                link(nc.vector.tensor_tensor(out=diff[:, :], in0=even, in1=odd, op=ALU.subtract), False)
                link(nc.vector.tensor_tensor(out=mean[:, :], in0=even, in1=odd, op=ALU.add), False)
                link(nc.vector.tensor_tensor(out=var[:, :], in0=stats[:, :, 2], in1=stats[:, :, 5], op=ALU.add))
                link(nc.vector.tensor_tensor(out=diff[:, :], in0=diff[:, :], in1=diff[:, :], op=ALU.mult), False)
                link(nc.vector.tensor_scalar(var[:, :], var[:, :], 1.0 / D, EPS, ALU.mult, ALU.add), False)
                link(nc.vector.tensor_scalar(mean[:, :], mean[:, :], 0.5, None, ALU.mult))
                nc.vector.scalar_tensor_tensor(out=var[:, :], in0=diff[:, :], scalar=0.25, in1=var[:, :],
                                               op0=ALU.mult, op1=ALU.add).then_inc(S["var_ready"], 1)
                dve.wait_ge(S["rstd_ready"], value(seg, n, "rstd_ready", k))
                for b in range(CB):
                    last = nc.vector.tensor_scalar(dst[:, b, :], src[:, b, :], mean[:, b:b + 1], rstd[:, b:b + 1],
                                                   ALU.subtract, ALU.mult)
                last.then_inc(S[done], 1)

            def run(seg, n, k, stage):
                kind = stage[0]
                if kind in ("gH1", "gY", "T", "O"):
                    dve.wait_ge(S["for_dve"], value(seg, n, "for_dve", k))
                    half = seg.half(k)
                    whole = ps[:, half, :, :].rearrange("d q (b t) -> d (q b) t", t=T)
                if kind == "gH1":
                    nc.vector.tensor_tensor(out=h1[:, :, :], in0=whole,
                                            in1=neg_bias1[:, :].unsqueeze(1).broadcast_to([D, CB, T]),
                                            op=ALU.max).then_inc(S["h1_ready"], 1)
                elif kind == "gY":
                    nc.vector.tensor_tensor(out=y[:, :, :], in0=whole,
                                            in1=bias2[:, :].unsqueeze(1).broadcast_to([T, CB, D]),
                                            op=ALU.add).then_inc(S["y_ready"], 1)
                elif kind == "T":
                    b0 = stage[1] * SB
                    dve.wait_ge(S["xr_loaded"], value(seg, n, "xr_loaded"))
                    nc.vector.tensor_tensor(out=u[:, b0:b0 + SB, :], in0=whole[:, 0:SB, :],
                                            in1=xr[:, b0:b0 + SB, :], op=ALU.add).then_inc(S["u_ready"], 1)
                elif kind == "norm1":
                    dve.wait_ge(S["u_ready"], value(seg, n, "u_ready", k))
                    normalise(seg, n, k, u, xn, "xn_ready")
                elif kind == "O":
                    b0 = stage[1] * SB
                    dve.wait_ge(S["r_ready"], value(seg, n, "r_ready", k))
                    if seg.start["out_ready"] or n is not None:
                        dve.wait_ge(S["stored"], value(seg, n, "stored"))
                    nc.vector.tensor_tensor(out=v[:, b0:b0 + SB, :], in0=whole[:, 0:SB, :],
                                            in1=r[:, b0:b0 + SB, :], op=ALU.add).then_inc(S["v_ready"], 1)
                elif kind == "norm2":
                    dve.wait_ge(S["v_ready"], value(seg, n, "v_ready", k))
                    normalise(seg, n, k, v, v, "out_ready")
                elif kind == "L":
                    _, p, s, stream, part = stage
                    unit, w = lstm_index(seg, k) % 2, windows(stage)
                    gates = gate_list(stage)
                    g_ = [t[:, 0:w] for t in gate[unit]]
                    c, tc, h = cell[stream][:, 0:w], tanh_c[unit][:, 0:w], h_new[unit][:, 0:w]
                    acts = value(seg, n, "acts", k)
                    order = value(seg, n, "dve_order", k)
                    dve.wait_ge(S["acts"], acts - len(gates) + 2)
                    if s == 0:
                        nc.vector.tensor_tensor(out=c, in0=g_[GI], in1=g_[GG], op=ALU.mult).then_inc(S["c_ready"], 1)
                    else:
                        nc.vector.tensor_tensor(out=g_[GG], in0=g_[GI], in1=g_[GG],
                                                op=ALU.mult).then_inc(S["dve_order"], 1)
                        dve.wait_ge(S["acts"], acts - 1)
                        nc.vector.tensor_tensor(out=c, in0=g_[GF], in1=c, op=ALU.mult).then_inc(S["dve_order"], 1)
                        dve.wait_ge(S["dve_order"], order - 2)
                        nc.vector.tensor_tensor(out=c, in0=c, in1=g_[GG], op=ALU.add).then_inc(S["c_ready"], 1)
                    last_step = s == p - 1
                    if last_step:
                        hi, lo = positions(h_hi, stage), positions(h_lo, stage)
                    else:
                        hi, lo = shaped(prev_hi[stream], stage), shaped(prev_lo[stream], stage)
                    dve.wait_ge(S["acts"], acts)
                    dve.wait_ge(S["tanhc"], value(seg, n, "tanhc", k))
                    nc.vector.tensor_tensor(out=h, in0=g_[GO], in1=tc, op=ALU.mult).then_inc(S["dve_order"], 1)
                    dve.wait_ge(S["dve_order"], order - 1)
                    h = shaped(h_new[unit], stage)
                    nc.vector.tensor_copy(hi, h).then_inc(S["dve_order"], 1)
                    dve.wait_ge(S["dve_order"], order)
                    nc.vector.tensor_tensor(out=lo, in0=h, in1=hi, op=ALU.subtract).then_inc(S["h_done"], 1)

            walk(dve, run)

        @block.tensor
        def _(pe):
            pe.wait_ge(w_loaded, FIRST_LOADS)
            nc.tensor.matmul(ps[:, 0, 0, 0:T], bg0_rows[:, :], adj_sb[:, :], start=True, stop=True).then_inc(bias_ps, 1)
            pe.wait_ge(bias_made, 2)
            nc.tensor.matmul(ps[:, 1, 0, 0:D], bias1[:, :], wg1_sb[:, :], start=True, stop=True).then_inc(bias_ps, 1)
            pe.wait_ge(bias_made, 3)

            def free_half(seg, n, k):
                slot = seg.slots.index(k)
                if slot >= 2:
                    at = seg.slots[slot - 2]
                    name = READ_BY[seg.stages[at][0]]
                    pe.wait_ge(S[name], value(seg, n, name, at))
                elif seg.before:
                    prior = seg.before
                    name = READ_BY[prior.stages[prior.slots[slot - 2]][0]]
                    back = value(seg, n, name)
                    later = sum(adds(prior.stages[at]).get(name, 0) for at in prior.slots[slot - 2:][1:])
                    pe.wait_ge(S[name], back - later)

            def run(seg, n, k, stage):
                kind = stage[0]
                if kind in NO_PSUM:
                    return
                half = seg.half(k)
                free_half(seg, n, k)
                whole = ps[:, half, :, :].rearrange("d q (b t) -> d (q b) t", t=T)
                if kind == "gZ":
                    pe.wait_ge(S["xg_loaded"], value(seg, n, "xg_loaded", k))
                    for b in range(CB):
                        last = nc.tensor.matmul(whole[:, b, :], xg[:, b, :], adj_sb[:, :], start=True, stop=True)
                    last.then_inc(S["for_act"], 1)
                elif kind == "gH1":
                    pe.wait_ge(S["z_ready"], value(seg, n, "z_ready", k))
                    for q in range(4):
                        last = nc.tensor.matmul(ps[:, half, q, :], wg0_sb[:, :], z[:, 4 * q:4 * q + 4, :],
                                                start=True, stop=True)
                    last.then_inc(S["for_dve"], 1)
                elif kind == "gY":
                    pe.wait_ge(S["h1_ready"], value(seg, n, "h1_ready", k))
                    for b in range(CB):
                        last = nc.tensor.matmul(whole[:, b, :], h1[:, b, :], wg1_sb[:, :], start=True, stop=True)
                    last.then_inc(S["for_dve"], 1)
                elif kind == "gH2":
                    pe.wait_ge(S["y_ready"], value(seg, n, "y_ready", k))
                    for b in range(CB):
                        last = nc.tensor.matmul(whole[:, b, :], y[:, b, :], adj_sb[:, :], start=True, stop=True)
                    last.then_inc(S["for_act"], 1)
                elif kind == "T":
                    pe.wait_ge(S["h_done"], value(seg, n, "h_done") - (1 if stage[1] == 0 else 0))
                    for j in range(SB):
                        b = stage[1] * SB + j
                        nc.tensor.matmul(whole[:, j, :], h_hi[:, b, :], ident[:, :], start=True, stop=False)
                        last = nc.tensor.matmul(whole[:, j, :], h_lo[:, b, :], ident[:, :], start=False, stop=True)
                    last.then_inc(S["for_dve"], 1)
                elif kind == "K":
                    pe.wait_ge(S["xn_ready"], value(seg, n, "xn_ready", k))
                    for j in range(4):
                        last = nc.tensor.matmul(ps[:, half, j, 0:3 * T], xn[:, 4 * stage[1] + j, :],
                                                adj3[:, :, :].rearrange("s k t -> s (k t)"), start=True, stop=True)
                    last.then_inc(S["for_act"], 1)
                elif kind == "O":
                    b0 = stage[1] * SB
                    pe.wait_ge(S["zk_ready"], value(seg, n, "zk_ready", k) - (2 if stage[1] == 0 else 0))
                    for j in range(SB):
                        for part in range(3):
                            last = nc.tensor.matmul(whole[:, j, :], zk[:, b0 + j, part, :], wl1_sb[:, part, :],
                                                    start=part == 0, stop=part == 2)
                    last.then_inc(S["for_dve"], 1)
                elif kind == "L":
                    _, p, s, stream, part = stage
                    gates = gate_list(stage)
                    if p == 1:
                        pe.wait_ge(S["h2_ready"], value(seg, n, "h2_ready"))
                        for g in gates:
                            nc.tensor.matmul(ps[:, half, g, :], wih_sb[:, 0, g, :], positions(h2, stage),
                                             start=True, stop=True).then_inc(S["gates"], 1)
                        return
                    if s == 0:
                        before = [j for j in range(k) if seg.stages[j][0] == "L" and seg.stages[j][3] == stream][-1]
                        pe.wait_ge(S["h_done"], value(seg, n, "h_done", before))
                    x_hi, x_lo = positions(h_hi, stage), positions(h_lo, stage)
                    w_hi, w_lo = wih_hi[:, p - 2, :, :], wih_lo[:, p - 2, :, :]
                    for g in gates:
                        o = shaped(ps[:, half, g, :], stage)
                        nc.tensor.matmul(o, w_hi[:, g, :], x_hi, start=True, stop=False)
                        nc.tensor.matmul(o, w_hi[:, g, :], x_lo, start=False, stop=False)
                        last = nc.tensor.matmul(o, w_lo[:, g, :], x_hi, start=False, stop=s == 0)
                        if s == 0:
                            last.then_inc(S["gates"], 1)
                    if s > 0:
                        before = find(seg, k, "L", p, s - 1, stream, 0)
                        pe.wait_ge(S["h_done"], value(seg, n, "h_done", before))
                        x_hi, x_lo = shaped(prev_hi[stream], stage), shaped(prev_lo[stream], stage)
                        w_hi, w_lo = whh_hi[:, p - 2, :, :], whh_lo[:, p - 2, :, :]
                        for g in gates:
                            o = shaped(ps[:, half, g, :], stage)
                            nc.tensor.matmul(o, w_hi[:, g, :], x_hi, start=False, stop=False)
                            nc.tensor.matmul(o, w_hi[:, g, :], x_lo, start=False, stop=False)
                            nc.tensor.matmul(o, w_lo[:, g, :], x_hi, start=False,
                                             stop=True).then_inc(S["gates"], 1)

            pe.wait_ge(masks_made, 6)
            pe.wait_ge(split_done, 6)
            pe.wait_ge(more_loaded, MORE_LOADS)
            walk(pe, run)


def kernel(**inputs):
    import numpy as np
    import concourse.bacc as bacc
    from concourse.bass_utils import run_bass_kernel_spmd

    def f(a):
        return np.asarray(a)

    ih, hh = f(inputs["L0_gnn_Wih"]), f(inputs["L0_gnn_Whh"])
    rows = lambda a: np.broadcast_to(f(a)[None, :], (T, D))
    arrays = {
        "x": f(inputs["x"]).transpose(1, 0, 2),
        "adj_t": f(inputs["adj"]).T,
        "w_ih": ih.reshape(LEVELS, 4, D, D).transpose(3, 0, 1, 2),
        "w_hh": hh.reshape(LEVELS, 4, D, D)[1:].transpose(3, 0, 1, 2),
        "b_ih": f(inputs["L0_gnn_bih"]).reshape(LEVELS, 4, D).transpose(2, 0, 1),
        "b_hh": f(inputs["L0_gnn_bhh"]).reshape(LEVELS, 4, D).transpose(2, 0, 1),
        "wg0": f(inputs["L0_gnn_Wg0"]),
        "bg0": rows(inputs["L0_gnn_bg0"]),
        "wg1": f(inputs["L0_gnn_Wg1"]),
        "bg1": rows(inputs["L0_gnn_bg1"]),
        "w_l1": f(inputs["L1_gnn_W"]).transpose(1, 0, 2),
        "b_l1": rows(inputs["L1_gnn_bias"]),
    }
    nc = bacc.Bacc("TRN2", target_bir_lowering=False, num_devices=1)
    feeds, aps = {}, []
    for name, a in arrays.items():
        feeds[name] = np.ascontiguousarray(a)
        aps.append(nc.dram_tensor(name, a.shape, mybir.dt.float32, kind="ExternalInput").ap())
    out = nc.dram_tensor("out", (T, B, D), mybir.dt.float32, kind="ExternalOutput").ap()
    build(nc, *aps, out)
    got = run_bass_kernel_spmd(nc, [feeds], core_ids=[0]).results[0]["out"]
    return got.transpose(1, 0, 2)
```

```python
import concourse.bass as bass
from concourse import mybir
from contextlib import ExitStack

B, T, D = 128, 128, 128
LEVELS = 4
CB = 16
CHUNKS = B // CB
CT = CB * T
STREAMS = 2
SB = CB // STREAMS
BANK = 512
WSCALE = 64.0
EPS = 1e-5
GI, GF, GG, GO = range(4)


def lstm(p, s, stream, *between):
    stream, part = stream if p == 1 else (stream, 0)
    return [("L", p, s, stream, part), *between, ("H", p, s, stream, part)]


def gate_list(stage):
    return (GG, GI, GO) if stage[2] == 0 else (GG, GI, GF, GO)


GCN_STAGES = ("gZ", "gH1", "gY", "gH2", "egZ", "egH1", "egY", "egH2", "loadx")
LSTM_STAGES = ("L", "H", "loadr", "pad")

TURN = (
    lstm(1, 0, (0, 0), ("T", 0, 8), ("eT", 0, 8)) + lstm(1, 0, (0, 1), ("T", 8, 8), ("eT", 8, 8))
    + [("loadr",), ("gZ",), ("egZ",), ("loadx",)] + lstm(1, 0, (1, 0), ("stats1", 0, 4))
    + lstm(1, 0, (1, 1), ("stats1", 4, 4)) + [("gH1",), ("egH1",)]
    + lstm(2, 0, 0, ("stats1", 8, 4)) + [("stats1", 12, 4), ("var1", 0, 16)]
    + lstm(2, 0, 1) + [("shift1", 0, 16), ("gY",), ("egY",)]
    + lstm(2, 1, 0, ("apply1", 0, 2)) + [("apply1", 2, 2), ("apply1", 4, 2)]
    + lstm(2, 1, 1, ("apply1", 6, 2), ("split", 0, 4)) + [("apply1", 8, 2)]
    + lstm(3, 0, 0, ("apply1", 10, 2), ("split", 4, 4)) + [("K", 0, 4), ("eK", 0, 4)]
    + lstm(3, 0, 1, ("apply1", 12, 2), ("split", 8, 4)) + [("apply1", 14, 2), ("K", 4, 4), ("eK", 4, 4)]
    + lstm(3, 1, 0, ("split", 12, 4)) + [("K", 8, 4), ("eK", 8, 4)]
    + lstm(3, 1, 1, ("bias", 0, 8)) + [("K", 12, 4), ("eK", 12, 4)]
    + lstm(3, 2, 0, ("bias", 8, 8)) + [("O", 0, 4), ("eO", 0, 4)]
    + lstm(3, 2, 1, ("stats2", 0, 4)) + [("O", 4, 4), ("eO", 4, 4), ("pad",)]
    + lstm(4, 0, 0, ("stats2", 4, 4)) + [("O", 8, 4), ("eO", 8, 4)]
    + lstm(4, 0, 1, ("stats2", 8, 4)) + [("O", 12, 4), ("eO", 12, 4)]
    + lstm(4, 1, 0, ("stats2", 12, 4)) + [("var2", 0, 16)] + lstm(4, 1, 1) + [("shift2", 0, 16), ("gH2",), ("egH2",)]
    + lstm(4, 2, 0, ("apply2", 0, 2)) + [("apply2", 2, 2)] + lstm(4, 2, 1, ("apply2", 4, 2)) + [("apply2", 6, 2)]
    + lstm(4, 3, 0, ("apply2", 8, 2)) + [("apply2", 10, 2)]
    + lstm(4, 3, 1, ("apply2", 12, 2)) + [("apply2", 14, 2), ("store", 0, 16)])


TURN = [
    ('L', 1, 0, 0, 0),
    ('T', 0, 8),
    ('eT', 0, 8),
    ('H', 1, 0, 0, 0),
    ('L', 1, 0, 0, 1),
    ('T', 8, 8),
    ('eT', 8, 8),
    ('H', 1, 0, 0, 1),
    ('L', 1, 0, 1, 0),
    ('stats1', 8, 2),
    ('stats1', 14, 2),
    ('gZ',),
    ('stats1', 0, 4),
    ('egZ',),
    ('stats1', 10, 2),
    ('H', 1, 0, 1, 0),
    ('L', 1, 0, 1, 1),
    ('loadx',),
    ('stats1', 12, 2),
    ('stats1', 4, 2),
    ('stats1', 6, 2),
    ('H', 1, 0, 1, 1),
    ('L', 2, 0, 0, 0),
    ('gH1',),
    ('egH1',),
    ('var1', 0, 16),
    ('H', 2, 0, 0, 0),
    ('L', 2, 0, 1, 0),
    ('H', 2, 0, 1, 0),
    ('shift1', 0, 16),
    ('L', 2, 1, 0, 0),
    ('apply1', 0, 2),
    ('apply1', 6, 2),
    ('apply1', 2, 1),
    ('H', 2, 1, 0, 0),
    ('apply1', 3, 1),
    ('L', 2, 1, 1, 0),
    ('apply1', 8, 4),
    ('split', 0, 4),
    ('H', 2, 1, 1, 0),
    ('loadr',),
    ('apply1', 4, 1),
    ('L', 3, 0, 0, 0),
    ('gY',),
    ('egY',),
    ('K', 0, 4),
    ('apply1', 5, 1),
    ('H', 3, 0, 0, 0),
    ('split', 4, 4),
    ('eK', 0, 4),
    ('apply1', 14, 2),
    ('L', 3, 0, 1, 0),
    ('apply1', 12, 2),
    ('H', 3, 0, 1, 0),
    ('L', 3, 1, 0, 0),
    ('K', 4, 4),
    ('split', 8, 8),
    ('eK', 4, 4),
    ('H', 3, 1, 0, 0),
    ('bias', 0, 16),
    ('L', 3, 1, 1, 0),
    ('H', 3, 1, 1, 0),
    ('L', 3, 2, 0, 0),
    ('O', 0, 4),
    ('eO', 0, 4),
    ('H', 3, 2, 0, 0),
    ('L', 3, 2, 1, 0),
    ('K', 8, 4),
    ('eK', 8, 4),
    ('O', 4, 4),
    ('eO', 4, 4),
    ('H', 3, 2, 1, 0),
    ('L', 4, 0, 0, 0),
    ('stats2', 0, 2),
    ('stats2', 2, 2),
    ('O', 8, 4),
    ('stats2', 4, 2),
    ('stats2', 6, 2),
    ('eO', 8, 4),
    ('L', 4, 0, 1, 0),
    ('H', 4, 0, 0, 0),
    ('H', 4, 0, 1, 0),
    ('K', 12, 4),
    ('stats2', 10, 2),
    ('eK', 12, 4),
    ('L', 4, 1, 0, 0),
    ('O', 12, 4),
    ('stats2', 8, 2),
    ('H', 4, 1, 0, 0),
    ('eO', 12, 4),
    ('stats2', 12, 2),
    ('stats2', 14, 2),
    ('var2', 0, 16),
    ('L', 4, 1, 1, 0),
    ('H', 4, 1, 1, 0),
    ('shift2', 0, 16),
    ('pad',),
    ('L', 4, 2, 0, 0),
    ('apply2', 8, 1),
    ('apply2', 0, 2),
    ('H', 4, 2, 0, 0),
    ('apply2', 4, 2),
    ('L', 4, 2, 1, 0),
    ('apply2', 7, 1),
    ('apply2', 2, 1),
    ('H', 4, 2, 1, 0),
    ('L', 4, 3, 0, 0),
    ('apply2', 3, 1),
    ('apply2', 15, 1),
    ('apply2', 6, 1),
    ('gH2',),
    ('egH2',),
    ('apply2', 10, 1),
    ('H', 4, 3, 0, 0),
    ('L', 4, 3, 1, 0),
    ('apply2', 9, 1),
    ('apply2', 11, 1),
    ('apply2', 12, 1),
    ('apply2', 13, 1),
    ('apply2', 14, 1),
    ('store', 0, 16),
    ('H', 4, 3, 1, 0),
]


def body(gcn, post, load=True):
    return [s for s in TURN if s[0] in LSTM_STAGES or (gcn if s[0] in GCN_STAGES else post)
            if load or s[0] != "loadx"]


PROLOGUE = [("loadx",), ("gZ",), ("egZ",), ("loadx",), ("gH1",), ("egH1",), ("gY",), ("egY",), ("gH2",), ("egH2",),
            ("pad",)]


def epilogue():
    first = [[("eT", b, 8), ("stats1", b, 4), ("stats1", b + 4, 4), ("var1", b, 8)] for b in (0, 8)]
    second = [[("shift1", b, 8)] + [st for c in (b, b + 4) for st in
              (("apply1", c, 2), ("applyd1", c + 2, 2), ("split", c, 4), ("K", c, 4), ("eK", c, 4))] for b in (0, 8)]
    third = [[("bias", b, 8)] + [st for c in (b, b + 4) for st in (("O", c, 4), ("eO", c, 4), ("stats2", c, 4))]
             + [("var2", b, 8)] for b in (0, 8)]
    fourth = [[("shift2", b, 8)] + [st for c in (b, b + 4) for st in (("apply2", c, 2), ("applyd2", c + 2, 2))]
              + [("store", b, 8)] for b in (0, 8)]
    return ([("T", 0, 8), ("T", 8, 8)] + first[0] + first[1] + second[0] + second[1]
            + third[0] + third[1] + fourth[0] + fourth[1])


EPILOGUE = epilogue()

EPILOGUE = [
    ('T', 0, 4),
    ('eT', 0, 4),
    ('stats1', 0, 4),
    ('T', 4, 4),
    ('var1', 0, 4),
    ('eT', 4, 4),
    ('T', 8, 4),
    ('stats1', 4, 4),
    ('T', 12, 4),
    ('shift1', 0, 4),
    ('applyd1', 0, 1),
    ('apply1', 1, 1),
    ('var1', 4, 4),
    ('eT', 8, 4),
    ('apply1', 2, 2),
    ('hi', 0, 4),
    ('shift1', 4, 4),
    ('lo', 0, 4),
    ('apply1', 4, 1),
    ('applyd1', 5, 1),
    ('applyd1', 6, 2),
    ('split', 4, 4),
    ('stats1', 8, 4),
    ('var1', 8, 4),
    ('eT', 12, 4),
    ('stats1', 14, 2),
    ('K', 0, 4),
    ('shift1', 8, 4),
    ('stats1', 12, 2),
    ('eK', 0, 4),
    ('K', 4, 4),
    ('apply1', 11, 1),
    ('applyd1', 8, 2),
    ('O', 0, 4),
    ('bias', 0, 8),
    ('apply1', 10, 1),
    ('split', 8, 4),
    ('var1', 12, 4),
    ('shift1', 12, 4),
    ('eK', 4, 4),
    ('apply1', 12, 4),
    ('O', 4, 4),
    ('K', 8, 4),
    ('hi', 12, 4),
    ('pbias', 8, 4),
    ('eO', 0, 4),
    ('eO', 4, 4),
    ('lo', 12, 4),
    ('stats2', 0, 8),
    ('var2', 0, 4),
    ('bias', 12, 4),
    ('shift2', 0, 4),
    ('K', 12, 4),
    ('eK', 8, 4),
    ('eK', 12, 4),
    ('O', 8, 4),
    ('var2', 4, 4),
    ('eO', 8, 4),
    ('apply2', 0, 4),
    ('stats2', 8, 4),
    ('shift2', 4, 4),
    ('O', 12, 4),
    ('var2', 8, 4),
    ('eO', 12, 4),
    ('stats2', 12, 4),
    ('shift2', 8, 4),
    ('apply2', 4, 2),
    ('apply2', 6, 2),
    ('var2', 12, 4),
    ('shift2', 12, 4),
    ('store', 0, 8),
    ('applyd2', 12, 4),
    ('apply2', 8, 4),
    ('store', 8, 8),
]


BANKS = {"gZ": 4, "gH1": 4, "gY": 4, "gH2": 4, "T": None, "K": 4, "O": None, "L": None}


def aligned(stage):
    return stage[0] != "L" and banks_of(stage) > 1


def banks_of(stage):
    kind = stage[0]
    return BANKS[kind] or (len(gate_list(stage)) if kind == "L" else stage[2] * T // BANK)



ADDS = {
    "loadx": {"xg_loaded0": 16, "xg_loaded1": 16},
    "loadr": {"xr_loaded": 16},
    "gZ": {"for_act": 2},
    "egZ": {"z_ready": 2},
    "gH1": {"for_dve": 2},
    "egH1": {"h1_ready": 2},
    "gY": {"for_dve": 2},
    "egY": {"y_ready": 2},
    "gH2": {"for_act": 2},
    "egH2": {"h2_hi_ready": 2, "h2_ready": 2},
    "T": {"for_dve": 1},
    "eT": {"u_ready": 1},
    "K": {"for_act": 1},
    "eK": {"zk_ready": 2},
    "O": {"for_dve": 1},
    "eO": {"v_ready": 1},
    "stats1": {"stats_ready": 1},
    "stats2": {"stats_ready": 1},
    "var1": {"var_ready": 1, "rstd_ready": 1, "dve_order": 5},
    "var2": {"var_ready": 1, "rstd_ready": 1, "dve_order": 5},
    "shift1": {"shift_ready": 1},
    "shift2": {"shift_ready": 1},
    "apply1": {"xn_ready": 1},
    "applyd1": {"xn_dve": 1},
    "apply2": {"out_ready": 1},
    "applyd2": {"out_dve": 1},
    "bias": {"r_ready": 1},
    "split": {"dve_order": 1, "parts_ready": 1},
    "hi": {"hi_ready": 1},
    "lo": {"parts_ready": 1},
    "pbias": {"r_pool": 1},
    "store": {"stored": 16},
    "pad": {},
    "H": {"tanhc": 1, "h_done": 1, "dve_order": 2},
}
READ_BY = {"gZ": "z_ready", "gH1": "h1_ready", "gY": "y_ready", "gH2": "h2_ready", "T": "u_ready",
           "K": "zk_ready", "O": "v_ready", "L": "acts"}


DONE = {"split": "parts_ready", "hi": "hi_ready", "lo": "parts_ready", "pbias": "r_pool",
        "eT": "u_ready", "eK": "zk_ready", "eO": "v_ready", "bias": "r_ready", "shift1": "shift_ready",
        "shift2": "shift_ready", "apply1": "xn_ready", "applyd1": "xn_dve", "apply2": "out_ready",
        "applyd2": "out_dve"}


def adds(stage):
    if stage[0] == "L":
        n = len(gate_list(stage))
        return {"gates": n, "acts": n, "c_ready": 1, "dve_order": 2 if stage[2] else 0}
    return ADDS[stage[0]]


NAMES = sorted({n for a in ADDS.values() for n in a} | set(adds(("L", 1, 1, 0, 0))))


class Segment:

    def __init__(self, stages, turns, chunk, before):
        self.stages, self.turns, self.chunk = stages, turns, chunk
        self.start = before.end() if before else dict.fromkeys(NAMES, 0)
        self.before = before
        self.through = []
        now = dict(self.start)
        for stage in stages:
            for name, n in adds(stage).items():
                now[name] += n
            self.through.append(dict(now))
        self.per_turn = {n: now[n] - self.start[n] for n in NAMES}
        self.banks, self.users = {}, [[] for _ in range(8)]
        at = 0
        for skip in range(8):
            at = 0
            for stage in stages:
                if stage[0] == "pad":
                    at += skip
                elif stage[0] in BANKS:
                    at += (aligned(stage) and at % 2) + banks_of(stage)
            if at % 8 == 0 or ("pad",) not in stages:
                break
        at = 0
        for k, stage in enumerate(stages):
            if stage[0] == "pad":
                at += skip
            if stage[0] not in BANKS:
                continue
            n = banks_of(stage)
            at += aligned(stage) and at % 2
            self.banks[k] = [(at + j) % 8 for j in range(n)]
            for j, bank in enumerate(self.banks[k]):
                self.users[bank].append((k, j))
            at += n

    def end(self):
        return {n: self.start[n] + self.turns * self.per_turn[n] for n in NAMES}

    def read(self, k, j):
        kind, *of = self.stages[k]
        name, by = READ_BY[kind], k if kind == "L" else self.stages.index(("e" + kind, *of))
        return name, self.through[by][name] - adds(self.stages[by])[name] + 1 + (j if kind == "L" else j // 2)

    def last_reads(self, bank):
        if not self.users[bank]:
            return {}
        name, at = self.read(*self.users[bank][-1])
        return {name: self.start[name] + self.per_turn[name] - at}

    def free(self, k, j):
        bank = self.banks[k][j]
        turn = self.users[bank].index((k, j))
        if turn:
            return [self.read(*self.users[bank][turn - 1])]
        waits = {}
        for seg in ([self.before] if self.before else []) + ([self] if self.turns > 1 else []):
            for name, short in seg.last_reads(bank).items():
                waits[name] = min(short, waits.get(name, short))
        return [(name, self.start[name] - short) for name, short in sorted(waits.items())]


def make_segments():
    segs = [Segment(PROLOGUE, 1, -1, None)]
    for stages, turns in ((body(True, False), 1), (body(True, True), CHUNKS - 3), (body(True, True, False), 1),
                          (body(False, True), 1), (EPILOGUE, 1)):
        chunk = sum(seg.turns for seg in segs) - 1
        segs.append(Segment(stages, turns, chunk, segs[-1]))
    return segs


def build(nc, x, adj_t, w_ih, w_hh, b_ih, b_hh, wg0, bg0, wg1, bg1, w_l1, b_l1, out):
    fp32, fp32r, fp16 = mybir.dt.float32, mybir.dt.float32r, mybir.dt.float16
    ALU, ACT = mybir.AluOpType, mybir.ActivationFunctionType
    segments = make_segments()
    ctx = ExitStack()
    with ctx:
        def sb(name, shape, dt=fp32):
            return ctx.enter_context(nc.sbuf_tensor(name, shape, dt))

        def sem(name):
            return ctx.enter_context(nc.semaphore(name))

        adj_sb = sb("adj_sb", [T, T])
        adj3 = sb("adj3", [T, 3, T])
        adj3_hi = sb("adj3_hi", [T, 3, T], fp32r)
        adj3_lo = sb("adj3_lo", [T, 3, T], fp32r)
        wg0_sb = sb("wg0_sb", [D, D])
        wg1_sb = sb("wg1_sb", [D, D])
        wl1_sb = sb("wl1_sb", [D, 3, D])
        wih_sb = sb("wih_sb", [D, LEVELS, 4, D])
        whh_sb = sb("whh_sb", [D, LEVELS - 1, 4, D])
        w1_hi = sb("w1_hi", [D, 4, D], fp32r)
        w1_lo = sb("w1_lo", [D, 4, D], fp32r)
        wih_hi = sb("wih_hi", [D, LEVELS - 1, 4, D], fp16)
        wih_lo = sb("wih_lo", [D, LEVELS - 1, 4, D], fp16)
        whh_hi = sb("whh_hi", [D, LEVELS - 1, 4, D], fp16)
        whh_lo = sb("whh_lo", [D, LEVELS - 1, 4, D], fp16)
        bih_sb = sb("bih_sb", [D, LEVELS, 4])
        bhh_sb = sb("bhh_sb", [D, LEVELS, 4])
        gate_bias = sb("gate_bias", [D, LEVELS, 4])
        bg0_rows = sb("bg0_rows", [T, D])
        bg1_rows = sb("bg1_rows", [T, D])
        bl1_rows = sb("bl1_rows", [T, D])
        bias1 = sb("bias1", [D, T])
        neg_bias1 = sb("neg_bias1", [D, T])
        bias2 = sb("bias2", [T, D])
        ident = sb("ident", [D, D], fp16)
        minus_half = sb("minus_half", [T, CB])
        xg = sb("xg", [T, CB, D])
        xr = sb("xr", [T, CB, D])
        z = sb("z", [D, CB, T])
        h1 = sb("h1", [D, CB, T])
        y = sb("y", [T, CB, D])
        h2_hi = sb("h2_hi", [D, CB, T], fp32r)
        h2_lo = sb("h2_lo", [D, CB, T], fp32r)
        h_hi = sb("h_hi", [D, CB, T], fp16)
        h_lo = sb("h_lo", [D, CB, T], fp16)
        u = sb("u", [T, CB, D])
        xn = sb("xn", [T, CB, D])
        xn_hi = sb("xn_hi", [T, CB, D], fp32r)
        xn_lo = sb("xn_lo", [T, CB, D], fp32r)
        zk = sb("zk", [D, CB, 3, T])
        v = sb("v", [T, CB, D])
        stats = sb("stats", [T, CB, 6])
        mean = sb("mean", [T, CB])
        diff = sb("diff", [T, CB])
        var = sb("var", [T, CB])
        rstd = [sb(f"rstd{norm}", [T, CB]) for norm in (1, 2)]
        shift = [sb(f"shift{norm}", [T, CB]) for norm in (1, 2)]
        gate = [[sb(f"gate{n}_{g}", [D, BANK]) for g in range(4)] for n in range(2)]
        tanh_c = [sb(f"tanh_c{n}", [D, BANK]) for n in range(2)]
        h_new = [sb(f"h_new{n}", [D, BANK]) for n in range(2)]
        cell = [sb(f"cell{a}", [D, BANK]) for a in range(STREAMS)]
        prev_hi = [sb(f"prev_hi{a}", [D, BANK], fp16) for a in range(STREAMS)]
        prev_lo = [sb(f"prev_lo{a}", [D, BANK], fp16) for a in range(STREAMS)]
        ps = ctx.enter_context(nc.psum_tensor("ps", [128, 8, BANK], fp32))

        S = {name: sem(name) for name in NAMES}
        adj_loaded = sem("adj_loaded")
        bg0_loaded = sem("bg0_loaded")
        w_loaded = sem("w_loaded")
        level1_loaded = sem("level1_loaded")
        lstm_loaded = [sem(f"lstm_loaded{p}") for p in range(2, LEVELS + 1)]
        hi_made = sem("hi_made")
        lo_made = sem("lo_made")
        post_loaded = sem("post_loaded")
        masks_made = sem("masks_made")
        split_done = sem("split_done")
        bias_ps = sem("bias_ps")
        bias_made = sem("bias_made")

        def value(seg, n, name, k=None):
            at = seg.start[name] if k is None else seg.through[k][name]
            return at if n is None else n * seg.per_turn[name] + at

        def made(seg, n, k, b0, nb, *kinds):
            found = {}
            for at, (kind, *of) in enumerate(seg.stages[:k]):
                if kind in kinds and of[0] < b0 + nb and b0 < of[0] + of[1]:
                    name = DONE[kind]
                    found[name] = value(seg, n, name, at)
            assert found
            return found.items()

        def sums(seg, k, nb):
            bank = seg.banks[k][0]
            return ps[:, bank:bank + nb * T // BANK, :].rearrange("t q (b d) -> t (q b) d", d=D)

        def pair(seg, k, half=0):
            bank = seg.banks[k][2 * half]
            return ps[:, bank:bank + 2, :].rearrange("d q (b t) -> d (q b) t", t=T)

        def walk(eng, run, segs):
            for seg in segs:
                if seg.turns == 1:
                    for k, stage in enumerate(seg.stages):
                        run(seg, None, k, stage)
                else:
                    with eng.Fori(0, seg.turns) as n:
                        for k, stage in enumerate(seg.stages):
                            run(seg, n, k, stage)

        SPLIT_AT = {("L", 1, 0, 1, 0): 2, ("L", 2, 0, 0, 0): 3, ("L", 3, 0, 0, 0): 4}

        def weight_parts(p):
            return [[t[:, p - 2 + off, :, :].rearrange("k g n -> k (g n)") for t, off in
                     ((w, w is wih_sb), (hi, 0), (lo, 0))]
                    for w, hi, lo in ((wih_sb, wih_hi, wih_lo), (whh_sb, whh_hi, whh_lo))]

        def lstm_index(seg, k):
            return sum(s[0] == seg.stages[k][0] for s in seg.stages[:k])

        def unit_done(seg, n, k, back):
            return value(seg, n, "h_done") + lstm_index(seg, k) + 1 - back

        def windows(stage):
            return SB * (T // stage[1]) if stage[1] > 1 else BANK

        def positions(arr, stage):
            _, p, s, stream, part = stage
            if p == 1:
                b0 = stream * SB + part * (BANK // T)
                return arr[:, b0:b0 + BANK // T, :]
            n = T // p
            part_of = arr[:, stream * SB:(stream + 1) * SB, 0:n * p]
            return part_of.rearrange("h b (w s) -> h b w s", s=p)[:, :, :, s]

        def shaped(ap, stage):
            return ap[:, 0:windows(stage)].rearrange("h (b w) -> h b w", w=T // stage[1])

        block = ctx.enter_context(nc.Block())

        @block.sync
        def _(sp):
            def run(seg, n, k, stage):
                chunk = seg.chunk if n is None else n + seg.chunk
                if stage == ("loadx",):
                    ahead = 1 if k == 0 else 2
                    if k:
                        sp.wait_ge(S["for_act"], value(seg, n, "for_act", seg.stages.index(("gZ",))))
                    for half in range(2):
                        sp.dma_start(xg[:, half * SB:(half + 1) * SB, :],
                                     x[:, bass.ds((chunk + ahead) * CB + half * SB, SB), :]
                                     ).then_inc(S[f"xg_loaded{half}"], 16)
                elif stage == ("loadr",):
                    if seg.chunk > 0:
                        sp.wait_ge(S["u_ready"], value(seg, n, "u_ready", k))
                    sp.dma_start(xr[:, :, :], x[:, bass.ds(chunk * CB, CB), :]).then_inc(S["xr_loaded"], 16)
                elif stage[0] == "store":
                    b0, nb = stage[1:]
                    for name, at in made(seg, n, k, b0, nb, "apply2", "applyd2"):
                        sp.wait_ge(S[name], at)
                    sp.dma_start(out[:, bass.ds((chunk - 1) * CB + b0, nb), :], v[:, b0:b0 + nb, :]
                                 ).then_inc(S["stored"], 16)

            sp.dma_start(adj_sb[:, :], adj_t).then_inc(adj_loaded, 16)
            sp.dma_start(bg0_rows[:, :], bg0).then_inc(bg0_loaded, 16)
            run(segments[0], None, 0, segments[0].stages[0])
            for dst, src in ((wg1_sb[:, :], wg1), (bg1_rows[:, :], bg1), (wg0_sb[:, :], wg0)):
                sp.dma_start(dst, src).then_inc(w_loaded, 16)
            for dst, src in ((wih_sb[:, 0, :, :], w_ih[:, 0, :, :]), (bih_sb[:, :, :], b_ih), (bhh_sb[:, :, :], b_hh)):
                sp.dma_start(dst, src).then_inc(level1_loaded, 16)
            for p in range(1, LEVELS):
                sp.dma_start(wih_sb[:, p, :, :], w_ih[:, p, :, :]).then_inc(lstm_loaded[p - 1], 16)
                sp.dma_start(whh_sb[:, p - 1, :, :], w_hh[:, p - 1, :, :]).then_inc(lstm_loaded[p - 1], 16)
            run(segments[0], None, 3, segments[0].stages[3])
            for dst, src in ((wl1_sb[:, :, :], w_l1), (bl1_rows[:, :], b_l1)):
                sp.dma_start(dst, src).then_inc(post_loaded, 16)
            walk(sp, run, segments[1:])
            sp.wait_ge(S["stored"], segments[-1].end()["stored"])

        W_LOADS, LEVEL1_LOADS, LEVEL_LOADS, POST_LOADS = 3 * 16, 3 * 16, 2 * 16, 2 * 16

        @block.gpsimd
        def _(pool):
            nc.gpsimd.memset(ident[:, :], 0.0).then_inc(masks_made, 1)
            nc.gpsimd.memset(minus_half[:, :], -0.5).then_inc(masks_made, 1)
            pool.wait_ge(masks_made, 1)
            nc.gpsimd.affine_select(out=ident[:, :], in_=ident[:, :], compare_op=ALU.not_equal, fill=1.0,
                                    base=0, pattern=[[-1, D]], channel_multiplier=1).then_inc(masks_made, 1)
            pool.wait_ge(adj_loaded, 16)
            for part, (op, sign) in enumerate(((ALU.is_equal, 1), (ALU.is_gt, 1), (ALU.is_gt, -1))):
                nc.gpsimd.affine_select(out=adj3[:, part, :], in_=adj_sb[:, :], compare_op=op, fill=0.0,
                                        base=0, pattern=[[-sign, T]],
                                        channel_multiplier=sign).then_inc(masks_made, 1)

            def run(seg, n, k, stage):
                if stage[0] in ("var1", "var2"):
                    pool.wait_ge(S["var_ready"], value(seg, n, "var_ready", k))
                    some = slice(stage[1], stage[1] + stage[2])
                    nc.gpsimd.tensor_tensor(out=rstd[int(stage[0][-1]) - 1][:, some], in0=var[:, some],
                                            in1=minus_half[:, some],
                                            op=ALU.pow).then_inc(S["rstd_ready"], 1)

                elif stage[0] == "pbias":
                    b0, nb = stage[1:]
                    for name, at in made(seg, n, k, b0, nb, "split", "lo"):
                        pool.wait_ge(S[name], at)
                    nc.gpsimd.tensor_tensor(out=xn[:, b0:b0 + nb, :], in0=xn[:, b0:b0 + nb, :],
                                            in1=bl1_rows[:, :].unsqueeze(1).broadcast_to([T, nb, D]),
                                            op=ALU.add).then_inc(S["r_pool"], 1)

            pool.wait_ge(masks_made, 6)
            walk(pool, run, segments)

        @block.scalar
        def _(act):
            def run(seg, n, k, stage):
                kind = stage[0]
                if seg is segments[1] and stage in SPLIT_AT:
                    act.wait_ge(lstm_loaded[SPLIT_AT[stage] - 2], LEVEL_LOADS)
                    for w, hi, lo in weight_parts(SPLIT_AT[stage]):
                        nc.scalar.activation(hi, w, ACT.Copy, scale=WSCALE).then_inc(hi_made, 1)
                if kind in ("egZ", "egH2", "eK"):
                    products = value(seg, n, "for_act", seg.stages.index((kind[1:], *stage[1:])))
                    for half in range(2):
                        if kind != "eK":
                            act.wait_ge(S["for_act"], products - 1 + half)
                        elif half == 0:
                            act.wait_ge(S["for_act"], products)
                        if kind == "egZ":
                            nc.scalar.activation(z[:, half * SB:(half + 1) * SB, :], pair(seg, seg.stages.index((kind[1:],)), half),
                                                 ACT.Copy).then_inc(S["z_ready"], 1)
                        elif kind == "egH2":
                            nc.scalar.activation(h2_hi[:, half * SB:(half + 1) * SB, :], pair(seg, seg.stages.index((kind[1:],)), half),
                                                 ACT.Relu).then_inc(S["h2_hi_ready"], 1)
                        else:
                            b0, bank = stage[1] + 2 * half, seg.banks[seg.stages.index(("K", *stage[1:]))][2 * half]
                            nc.scalar.activation(zk[:, b0:b0 + 2, :, :].rearrange("d b k t -> d b (k t)"),
                                                 ps[:, bank:bank + 2, 0:3 * T], ACT.Copy).then_inc(S["zk_ready"], 1)
                elif kind == "L":
                    _, p, s, stream, part = stage
                    unit, w = lstm_index(seg, k) % 2, windows(stage)
                    gates = gate_list(stage)
                    if not (seg.start["h_done"] == 0 and lstm_index(seg, k) < 2):
                        act.wait_ge(S["h_done"], unit_done(seg, n, k, 2))
                    ready = value(seg, n, "gates", k)
                    for j, g in enumerate(gates):
                        act.wait_ge(S["gates"], ready - len(gates) + 1 + j)
                        nc.scalar.activation(gate[unit][g][:, 0:w], ps[:, seg.banks[k][j], 0:w],
                                             ACT.Tanh if g == GG else ACT.Sigmoid,
                                             bias=gate_bias[:, p - 1, g:g + 1],
                                             scale=1.0 if p == 1 else 1.0 / WSCALE).then_inc(S["acts"], 1)
                elif kind == "H":
                    unit, w = lstm_index(seg, k) % 2, windows(stage)
                    act.wait_ge(S["c_ready"], value(seg, n, "c_ready", k))
                    nc.scalar.activation(tanh_c[unit][:, 0:w], cell[unit][:, 0:w],
                                         ACT.Tanh).then_inc(S["tanhc"], 1)
                elif kind in ("apply1", "apply2"):
                    src, dst, name = (u, xn, "xn_ready") if kind == "apply1" else (v, v, "out_ready")
                    b0, nb = stage[1:]
                    norm = int(kind[-1]) - 1
                    for other, at in made(seg, n, k, b0, nb, f"shift{norm + 1}"):
                        act.wait_ge(S[other], at)
                    for b in range(b0, b0 + nb):
                        last = nc.scalar.activation(dst[:, b, :], src[:, b, :], ACT.Identity,
                                                    bias=shift[norm][:, b:b + 1],
                                                    scale=rstd[norm][:, b:b + 1])
                    last.then_inc(S[name], 1)

                elif kind == "hi":
                    b0, nb = stage[1:]
                    for other, at in made(seg, n, k, b0, nb, "apply1", "applyd1"):
                        act.wait_ge(S[other], at)
                    nc.scalar.activation(xn_hi[:, b0:b0 + nb, :], xn[:, b0:b0 + nb, :],
                                         ACT.Copy).then_inc(S["hi_ready"], 1)

            walk(act, run, segments[:1])
            act.wait_ge(split_done, 1)
            walk(act, run, segments[1:])

        @block.vector
        def _(dve):
            dve.wait_ge(bias_ps, 1)
            nc.vector.tensor_copy(bias1[:, :], ps[:, 6, 0:T]).then_inc(bias_made, 1)
            nc.vector.tensor_scalar(neg_bias1[:, :], ps[:, 6, 0:T], -1.0, None, ALU.mult).then_inc(bias_made, 1)
            dve.wait_ge(bias_ps, 2)
            dve.wait_ge(w_loaded, W_LOADS)
            nc.vector.tensor_tensor(out=bias2[:, :], in0=ps[:, 7, 0:D], in1=bg1_rows[:, :],
                                    op=ALU.add).then_inc(bias_made, 1)
            dve.wait_ge(bias_made, 3)
            def split(src, hi, lo, count):
                nc.vector.tensor_copy(hi, src).then_inc(split_done, 1)
                dve.wait_ge(split_done, count)
                nc.vector.tensor_tensor(out=lo, in0=src, in1=hi.bitcast(fp32), op=ALU.subtract).then_inc(split_done, 1)

            def low_weights(p):
                dve.wait_ge(hi_made, 2 * (p - 1))
                for w, hi, lo in weight_parts(p):
                    nc.vector.scalar_tensor_tensor(out=lo, in0=w, scalar=WSCALE, in1=hi, op0=ALU.mult,
                                                   op1=ALU.subtract).then_inc(lo_made, 1)

            def variances(seg, n, k, b0, nb):
                base = value(seg, n, "dve_order", k) - 5
                count = [0]

                def link(ins, wait=True):
                    count[0] += 1
                    ins.then_inc(S["dve_order"], 1)
                    if wait:
                        dve.wait_ge(S["dve_order"], base + count[0])

                dve.wait_ge(S["stats_ready"], value(seg, n, "stats_ready", k))
                even, odd, in_even, in_odd = (stats[:, b0:b0 + nb, field] for field in (1, 4, 2, 5))
                d, m, q = (t[:, b0:b0 + nb] for t in (diff, mean, var))
                link(nc.vector.tensor_tensor(out=d, in0=even, in1=odd, op=ALU.subtract), False)
                link(nc.vector.tensor_tensor(out=m, in0=even, in1=odd, op=ALU.add), False)
                link(nc.vector.tensor_tensor(out=q, in0=in_even, in1=in_odd, op=ALU.add))
                link(nc.vector.tensor_tensor(out=d, in0=d, in1=d, op=ALU.mult), False)
                link(nc.vector.tensor_scalar(q, q, 1.0 / D, EPS, ALU.mult, ALU.add))
                nc.vector.scalar_tensor_tensor(out=q, in0=d, scalar=0.25, in1=q,
                                               op0=ALU.mult, op1=ALU.add).then_inc(S["var_ready"], 1)

            def run(seg, n, k, stage):
                kind = stage[0]
                if seg is segments[1] and stage in SPLIT_AT:
                    low_weights(SPLIT_AT[stage])
                if seg is segments[1] and stage == ("L", 4, 0, 0, 0):
                    dve.wait_ge(masks_made, 6)
                    flat = "s k t -> s (k t)"
                    split(adj3[:, :, :].rearrange(flat), adj3_hi[:, :, :].rearrange(flat),
                          adj3_lo[:, :, :].rearrange(flat), 4)
                    dve.wait_ge(post_loaded, POST_LOADS)
                if kind in ("egH1", "egY", "egH2", "eT", "eO"):
                    made_by = seg.stages.index((kind[1:], *stage[1:]))
                    products = value(seg, n, "for_dve", made_by)
                if kind in ("egH1", "egY"):
                    dst, tile, op, name = ((h1, neg_bias1, ALU.max, "h1_ready") if kind == "egH1" else
                                           (y, bias2, ALU.add, "y_ready"))
                    for half in range(2):
                        dve.wait_ge(S["for_dve"], products - 1 + half)
                        nc.vector.tensor_tensor(out=dst[:, half * SB:(half + 1) * SB, :],
                                                in0=pair(seg, made_by, half),
                                                in1=tile[:, :].unsqueeze(1).broadcast_to([128, SB, 128]),
                                                op=op).then_inc(S[name], 1)
                elif kind == "egH2":
                    for half in range(2):
                        dve.wait_ge(S["h2_hi_ready"], value(seg, n, "h2_hi_ready", k) - 1 + half)
                        some = slice(half * SB, (half + 1) * SB)
                        nc.vector.scalar_tensor_tensor(out=h2_lo[:, some, :], in0=pair(seg, made_by, half), scalar=0.0,
                                                       in1=h2_hi[:, some, :].bitcast(fp32), op0=ALU.max,
                                                       op1=ALU.subtract).then_inc(S["h2_ready"], 1)
                elif kind == "eT":
                    b0, nb = stage[1:]
                    dve.wait_ge(S["for_dve"], products)
                    dve.wait_ge(S["xr_loaded"], value(seg, n, "xr_loaded"))
                    nc.vector.tensor_tensor(out=u[:, b0:b0 + nb, :], in0=sums(seg, made_by, nb),
                                            in1=xr[:, b0:b0 + nb, :], op=ALU.add).then_inc(S["u_ready"], 1)
                elif kind == "eO":
                    b0, nb = stage[1:]
                    dve.wait_ge(S["for_dve"], products)
                    for name, at in made(seg, n, k, b0, nb, "bias", "pbias"):
                        dve.wait_ge(S[name], at)
                    if seg.start["out_ready"] or n is not None:
                        dve.wait_ge(S["stored"], value(seg, n, "stored"))
                    nc.vector.tensor_tensor(out=v[:, b0:b0 + nb, :], in0=sums(seg, made_by, nb),
                                            in1=xn[:, b0:b0 + nb, :], op=ALU.add).then_inc(S["v_ready"], 1)
                elif kind in ("stats1", "stats2"):
                    b0, nb = stage[1:]
                    for name, at in made(seg, n, k, b0, nb, "eT" if kind == "stats1" else "eO"):
                        dve.wait_ge(S[name], at)
                    for b in range(b0, b0 + nb):
                        last = nc.vector.bn_stats(stats[:, b, :], (u if kind == "stats1" else v)[:, b, :])
                    last.then_inc(S["stats_ready"], 1)
                elif kind in ("var1", "var2"):
                    variances(seg, n, k, *stage[1:])
                elif kind in ("shift1", "shift2"):
                    norm, some = int(kind[-1]) - 1, slice(stage[1], stage[1] + stage[2])
                    at = max(j for j in range(k) if seg.stages[j][0] == f"var{norm + 1}"
                             and seg.stages[j][1:] == stage[1:])
                    dve.wait_ge(S["rstd_ready"], value(seg, n, "rstd_ready", at))
                    nc.vector.scalar_tensor_tensor(out=shift[norm][:, some], in0=mean[:, some], scalar=-0.5,
                                                   in1=rstd[norm][:, some],
                                                   op0=ALU.mult, op1=ALU.mult).then_inc(S["shift_ready"], 1)
                elif kind in ("applyd1", "applyd2"):
                    b0, nb = stage[1:]
                    norm = int(kind[-1]) - 1
                    src, dst = ((u, xn), (v, v))[norm]
                    for name, at in made(seg, n, k, b0, nb, f"shift{norm + 1}"):
                        dve.wait_ge(S[name], at)
                    for b in range(b0, b0 + nb):
                        last = nc.vector.tensor_scalar(dst[:, b, :], src[:, b, :], rstd[norm][:, b:b + 1],
                                                       shift[norm][:, b:b + 1], ALU.mult, ALU.add)
                    last.then_inc(S[DONE[kind]], 1)
                elif kind == "split":
                    b0, nb = stage[1:]
                    for name, at in made(seg, n, k, b0, nb, "apply1", "applyd1"):
                        dve.wait_ge(S[name], at)
                    some = slice(b0, b0 + nb)
                    nc.vector.tensor_copy(xn_hi[:, some, :], xn[:, some, :]).then_inc(S["dve_order"], 1)
                    dve.wait_ge(S["dve_order"], value(seg, n, "dve_order", k))
                    nc.vector.tensor_tensor(out=xn_lo[:, some, :], in0=xn[:, some, :],
                                            in1=xn_hi[:, some, :].bitcast(fp32),
                                            op=ALU.subtract).then_inc(S["parts_ready"], 1)
                elif kind == "lo":
                    b0, nb = stage[1:]
                    for name, at in made(seg, n, k, b0, nb, "hi"):
                        dve.wait_ge(S[name], at)
                    some = slice(b0, b0 + nb)
                    nc.vector.tensor_tensor(out=xn_lo[:, some, :], in0=xn[:, some, :],
                                            in1=xn_hi[:, some, :].bitcast(fp32),
                                            op=ALU.subtract).then_inc(S["parts_ready"], 1)
                elif kind == "bias":
                    b0, nb = stage[1:]
                    for name, at in made(seg, n, k, b0, nb, "split", "lo"):
                        dve.wait_ge(S[name], at)
                    nc.vector.tensor_tensor(out=xn[:, b0:b0 + nb, :], in0=xn[:, b0:b0 + nb, :],
                                            in1=bl1_rows[:, :].unsqueeze(1).broadcast_to([T, nb, D]),
                                            op=ALU.add).then_inc(S["r_ready"], 1)
                elif kind in ("L", "H"):
                    _, p, s, stream, part = stage
                    unit, w = lstm_index(seg, k) % 2, windows(stage)
                    gates = gate_list(stage)
                    g_ = [t[:, 0:w] for t in gate[unit]]
                    c, tc, h = cell[unit][:, 0:w], tanh_c[unit][:, 0:w], h_new[unit][:, 0:w]
                    acts = value(seg, n, "acts", seg.stages.index(("L",) + stage[1:]))
                    order = value(seg, n, "dve_order", k)
                    if kind == "L":
                        dve.wait_ge(S["acts"], acts - len(gates) + 2)
                    if kind == "H":
                        pass
                    elif s == 0:
                        nc.vector.tensor_tensor(out=c, in0=g_[GI], in1=g_[GG], op=ALU.mult).then_inc(S["c_ready"], 1)
                    else:
                        nc.vector.tensor_tensor(out=g_[GG], in0=g_[GI], in1=g_[GG],
                                                op=ALU.mult).then_inc(S["dve_order"], 1)
                        dve.wait_ge(S["acts"], acts - 1)
                        nc.vector.tensor_tensor(out=c, in0=g_[GF], in1=c, op=ALU.mult).then_inc(S["dve_order"], 1)
                        dve.wait_ge(S["dve_order"], order)
                        nc.vector.tensor_tensor(out=c, in0=c, in1=g_[GG], op=ALU.add).then_inc(S["c_ready"], 1)
                    if kind == "L":
                        return
                    last_step = s == p - 1
                    if last_step:
                        hi, lo = positions(h_hi, stage), positions(h_lo, stage)
                    else:
                        hi, lo = shaped(prev_hi[stream], stage), shaped(prev_lo[stream], stage)
                    dve.wait_ge(S["acts"], acts)
                    dve.wait_ge(S["tanhc"], value(seg, n, "tanhc", k))
                    nc.vector.tensor_tensor(out=h, in0=g_[GO], in1=tc, op=ALU.mult).then_inc(S["dve_order"], 1)
                    dve.wait_ge(S["dve_order"], order - 1)
                    h = shaped(h_new[unit], stage)
                    nc.vector.tensor_copy(hi, h).then_inc(S["dve_order"], 1)
                    dve.wait_ge(S["dve_order"], order)
                    nc.vector.tensor_tensor(out=lo, in0=h, in1=hi, op=ALU.subtract).then_inc(S["h_done"], 1)

            walk(dve, run, segments[:1])
            dve.wait_ge(level1_loaded, LEVEL1_LOADS)
            nc.vector.tensor_tensor(out=gate_bias[:, :, :], in0=bih_sb[:, :, :], in1=bhh_sb[:, :, :],
                                    op=ALU.add).then_inc(split_done, 1)
            split(wih_sb[:, 0, :, :].rearrange("k g n -> k (g n)"), w1_hi[:, :, :].rearrange("k g n -> k (g n)"),
                  w1_lo[:, :, :].rearrange("k g n -> k (g n)"), 2)
            walk(dve, run, segments[1:])

        @block.tensor
        def _(pe):
            pe.wait_ge(adj_loaded, 16)
            pe.wait_ge(bg0_loaded, 16)
            nc.tensor.matmul(ps[:, 6, 0:T], bg0_rows[:, :], adj_sb[:, :], start=True, stop=True).then_inc(bias_ps, 1)

            def free(seg, n, k, j, count=1):
                waits = {}
                for jj in range(j, j + count):
                    for name, at in seg.free(k, jj):
                        waits[name] = max(at, waits.get(name, at))
                for name, at in waits.items():
                    pe.wait_ge(S[name], at if n is None else n * seg.per_turn[name] + at)

            def run(seg, n, k, stage):
                kind = stage[0]
                if kind not in BANKS:
                    return
                if seg is segments[1] and kind == "L" and stage[1] > 1 and stage[2:4] == (0, 0):
                    pe.wait_ge(lo_made, 2 * (stage[1] - 1))
                if seg is segments[2] and k == 0:
                    pe.wait_ge(post_loaded, POST_LOADS)
                    pe.wait_ge(split_done, 5)
                    pe.wait_ge(masks_made, 3)
                if kind == "gZ":
                    for half in range(2):
                        name = f"xg_loaded{half}"
                        pe.wait_ge(S[name], value(seg, n, name, k))
                        free(seg, n, k, 2 * half, 2)
                        for j in range(SB):
                            last = nc.tensor.matmul(pair(seg, k, half)[:, j, :], xg[:, half * SB + j, :],
                                                    adj_sb[:, :], start=True, stop=True)
                        last.then_inc(S["for_act"], 1)
                elif kind == "gH1":
                    if seg is segments[0]:
                        pe.wait_ge(w_loaded, W_LOADS)
                        pe.wait_ge(bias_made, 2)
                        nc.tensor.matmul(ps[:, 7, 0:D], bias1[:, :], wg1_sb[:, :], start=True,
                                         stop=True).then_inc(bias_ps, 1)
                        pe.wait_ge(bias_made, 3)
                    for half in range(2):
                        free(seg, n, k, 2 * half, 2)
                        pe.wait_ge(S["z_ready"], value(seg, n, "z_ready", seg.stages.index(("egZ",))) - 1 + half)
                        for q in (2 * half, 2 * half + 1):
                            last = nc.tensor.matmul(ps[:, seg.banks[k][q], :], wg0_sb[:, :], z[:, 4 * q:4 * q + 4, :],
                                                    start=True, stop=True)
                        last.then_inc(S["for_dve"], 1)
                elif kind == "gY":
                    for half in range(2):
                        free(seg, n, k, 2 * half, 2)
                        pe.wait_ge(S["h1_ready"], value(seg, n, "h1_ready", seg.stages.index(("egH1",))) - 1 + half)
                        for j in range(SB):
                            last = nc.tensor.matmul(pair(seg, k, half)[:, j, :], h1[:, half * SB + j, :],
                                                    wg1_sb[:, :], start=True, stop=True)
                        last.then_inc(S["for_dve"], 1)
                elif kind == "gH2":
                    for half in range(2):
                        free(seg, n, k, 2 * half, 2)
                        pe.wait_ge(S["y_ready"], value(seg, n, "y_ready", seg.stages.index(("egY",))) - 1 + half)
                        for j in range(SB):
                            last = nc.tensor.matmul(pair(seg, k, half)[:, j, :], y[:, half * SB + j, :],
                                                    adj_sb[:, :], start=True, stop=True)
                        last.then_inc(S["for_act"], 1)
                elif kind == "T":
                    b0, nb = stage[1:]
                    free(seg, n, k, 0, len(seg.banks[k]))
                    pe.wait_ge(S["h_done"], value(seg, n, "h_done") - (1 if b0 + nb <= SB else 0))
                    for j in range(nb):
                        o = sums(seg, k, nb)[:, j, :]
                        nc.tensor.matmul(o, h_hi[:, b0 + j, :], ident[:, :], start=True, stop=False)
                        last = nc.tensor.matmul(o, h_lo[:, b0 + j, :], ident[:, :], start=False, stop=True)
                    last.then_inc(S["for_dve"], 1)
                elif kind == "K":
                    b0, nb = stage[1:]
                    for name, at in made(seg, n, k, b0, nb, "split", "lo"):
                        pe.wait_ge(S[name], at)
                    a_hi, a_lo = (t[:, :, :].rearrange("s k t -> s (k t)") for t in (adj3_hi, adj3_lo))
                    for j in range(nb):
                        free(seg, n, k, j)
                        o = ps[:, seg.banks[k][j], 0:3 * T]
                        nc.tensor.matmul(o, xn_hi[:, b0 + j, :], a_hi, start=True, stop=False)
                        nc.tensor.matmul(o, xn_hi[:, b0 + j, :], a_lo, start=False, stop=False)
                        last = nc.tensor.matmul(o, xn_lo[:, b0 + j, :], a_hi, start=False, stop=True)
                    last.then_inc(S["for_act"], 1)
                elif kind == "O":
                    b0, nb = stage[1:]
                    free(seg, n, k, 0, len(seg.banks[k]))
                    for name, at in made(seg, n, k, b0, nb, "eK"):
                        pe.wait_ge(S[name], at)
                    for j in range(nb):
                        for part in range(3):
                            last = nc.tensor.matmul(sums(seg, k, nb)[:, j, :], zk[:, b0 + j, part, :],
                                                    wl1_sb[:, part, :], start=part == 0, stop=part == 2)
                    last.then_inc(S["for_dve"], 1)
                elif kind == "L":
                    _, p, s, stream, part = stage
                    gates = gate_list(stage)
                    if p == 1:
                        pe.wait_ge(S["h2_ready"], value(seg, n, "h2_ready") - 1 + stream)
                        for j, g in enumerate(gates):
                            free(seg, n, k, j)
                            o = ps[:, seg.banks[k][j], :]
                            x_hi, x_lo = positions(h2_hi, stage), positions(h2_lo, stage)
                            nc.tensor.matmul(o, w1_hi[:, g, :], x_hi, start=True, stop=False)
                            nc.tensor.matmul(o, w1_hi[:, g, :], x_lo, start=False, stop=False)
                            nc.tensor.matmul(o, w1_lo[:, g, :], x_hi, start=False,
                                             stop=True).then_inc(S["gates"], 1)
                        return
                    if s == 0:
                        pe.wait_ge(S["h_done"], unit_done(seg, n, k, 3 if p == 2 and stream == 0 else 2))
                    x_hi, x_lo = positions(h_hi, stage), positions(h_lo, stage)
                    w_hi, w_lo = wih_hi[:, p - 2, :, :], wih_lo[:, p - 2, :, :]
                    for j, g in enumerate(gates):
                        free(seg, n, k, j)
                        o = shaped(ps[:, seg.banks[k][j], :], stage)
                        nc.tensor.matmul(o, w_hi[:, g, :], x_hi, start=True, stop=False)
                        nc.tensor.matmul(o, w_hi[:, g, :], x_lo, start=False, stop=False)
                        last = nc.tensor.matmul(o, w_lo[:, g, :], x_hi, start=False, stop=s == 0)
                        if s == 0:
                            last.then_inc(S["gates"], 1)
                    if s > 0:
                        pe.wait_ge(S["h_done"], unit_done(seg, n, k, 2))
                        x_hi, x_lo = shaped(prev_hi[stream], stage), shaped(prev_lo[stream], stage)
                        w_hi, w_lo = whh_hi[:, p - 2, :, :], whh_lo[:, p - 2, :, :]
                        for j, g in enumerate(gates):
                            o = shaped(ps[:, seg.banks[k][j], :], stage)
                            nc.tensor.matmul(o, w_hi[:, g, :], x_hi, start=False, stop=False)
                            nc.tensor.matmul(o, w_hi[:, g, :], x_lo, start=False, stop=False)
                            nc.tensor.matmul(o, w_lo[:, g, :], x_hi, start=False,
                                             stop=True).then_inc(S["gates"], 1)

            walk(pe, run, segments[:1])
            pe.wait_ge(split_done, 3)
            walk(pe, run, segments[1:])


def kernel(**inputs):
    import numpy as np
    import concourse.bacc as bacc
    from concourse.bass_utils import run_bass_kernel_spmd

    def f(a):
        return np.asarray(a)

    ih, hh = f(inputs["L0_gnn_Wih"]), f(inputs["L0_gnn_Whh"])
    rows = lambda a: np.broadcast_to(f(a)[None, :], (T, D))
    arrays = {
        "x": f(inputs["x"]).transpose(1, 0, 2),
        "adj_t": f(inputs["adj"]).T,
        "w_ih": ih.reshape(LEVELS, 4, D, D).transpose(3, 0, 1, 2),
        "w_hh": hh.reshape(LEVELS, 4, D, D)[1:].transpose(3, 0, 1, 2),
        "b_ih": f(inputs["L0_gnn_bih"]).reshape(LEVELS, 4, D).transpose(2, 0, 1),
        "b_hh": f(inputs["L0_gnn_bhh"]).reshape(LEVELS, 4, D).transpose(2, 0, 1),
        "wg0": f(inputs["L0_gnn_Wg0"]),
        "bg0": rows(inputs["L0_gnn_bg0"]),
        "wg1": f(inputs["L0_gnn_Wg1"]),
        "bg1": rows(inputs["L0_gnn_bg1"]),
        "w_l1": f(inputs["L1_gnn_W"]).transpose(1, 0, 2),
        "b_l1": rows(inputs["L1_gnn_bias"]),
    }
    nc = bacc.Bacc("TRN2", target_bir_lowering=False, num_devices=1)
    feeds, aps = {}, []
    for name, a in arrays.items():
        feeds[name] = np.ascontiguousarray(a)
        aps.append(nc.dram_tensor(name, a.shape, mybir.dt.float32, kind="ExternalInput").ap())
    out = nc.dram_tensor("out", (T, B, D), mybir.dt.float32, kind="ExternalOutput").ap()
    build(nc, *aps, out)
    got = run_bass_kernel_spmd(nc, [feeds], core_ids=[0]).results[0]["out"]
    return got.transpose(1, 0, 2)
```

```python
import concourse.bass as bass
from concourse import mybir
from contextlib import ExitStack

B, T, D = 128, 128, 128
LEVELS = 4
CB = 16
CHUNKS = B // CB
STREAMS = 2
SB = CB // STREAMS
BANK = 512
WSCALE = 64.0
EPS = 1e-5
WARM_UP = 12
GI, GF, GG, GO = range(4)


def gate_list(stage):
    return (GG, GI, GO) if stage[2] == 0 else (GG, GI, GF, GO)


GCN_STAGES = ("gZ", "gH1", "gY", "gH2", "egZ", "egH1", "egY", "egH2", "loadx")
LSTM_STAGES = ("L", "H", "loadr", "pad")

TURN = [
    ("L", 1, 0, 0, 0), ("T", 0, 8), ("eT", 0, 8), ("H", 1, 0, 0, 0), ("stats1", 0, 2),
    ("L", 1, 0, 0, 1), ("T", 8, 8), ("eT", 8, 8),
    ("L", 1, 0, 1, 0), ("gZ",), ("stats1", 14, 2), ("stats1", 8, 2), ("stats1", 10, 2), ("H", 1, 0, 0, 1),
        ("stats1", 2, 2), ("loadx",), ("egZ",), ("H", 1, 0, 1, 0),
    ("L", 1, 0, 1, 1), ("stats1", 6, 2), ("stats1", 12, 2), ("H", 1, 0, 1, 1),
    ("L", 2, 0, 0, 0), ("stats1", 4, 2), ("gH1",), ("egH1",), ("var1", 0, 16), ("H", 2, 0, 0, 0),
    ("L", 2, 0, 1, 0), ("shift1", 0, 16), ("H", 2, 0, 1, 0),
    ("L", 2, 1, 0, 0), ("apply1", 6, 2), ("apply1", 2, 1), ("apply1", 0, 2), ("H", 2, 1, 0, 0), ("apply1", 3, 1),
    ("L", 2, 1, 1, 0), ("apply1", 8, 2), ("apply1", 11, 1), ("apply1", 10, 1), ("split", 0, 4), ("H", 2, 1, 1, 0),
    ("L", 3, 0, 0, 0), ("apply1", 12, 1), ("loadr",), ("gY",), ("K", 0, 4), ("egY",), ("apply1", 5, 1),
        ("apply1", 4, 1), ("apply1", 13, 1), ("H", 3, 0, 0, 0), ("eK", 0, 4), ("apply1", 14, 2), ("split", 4, 4),
    ("L", 3, 0, 1, 0), ("H", 3, 0, 1, 0),
    ("L", 3, 1, 0, 0), ("split", 8, 4), ("K", 4, 4), ("eK", 4, 4), ("split", 12, 4), ("H", 3, 1, 0, 0),
        ("bias", 0, 8), ("bias", 8, 8),
    ("L", 3, 1, 1, 0), ("H", 3, 1, 1, 0),
    ("L", 3, 2, 0, 0), ("O", 0, 4), ("eO", 0, 4), ("stats2", 0, 4), ("K", 8, 4), ("H", 3, 2, 0, 0), ("eK", 8, 4),
    ("L", 3, 2, 1, 0), ("H", 3, 2, 1, 0),
    ("L", 4, 0, 0, 0), ("O", 4, 4), ("eO", 4, 4), ("H", 4, 0, 0, 0), ("stats2", 4, 2), ("O", 8, 4),
    ("L", 4, 0, 1, 0), ("eO", 8, 4), ("H", 4, 0, 1, 0), ("stats2", 6, 2), ("K", 12, 4), ("eK", 12, 4),
        ("stats2", 10, 2),
    ("L", 4, 1, 0, 0), ("stats2", 8, 2), ("O", 12, 4), ("H", 4, 1, 0, 0), ("eO", 12, 4), ("stats2", 12, 2),
        ("stats2", 14, 2), ("var2", 0, 16),
    ("L", 4, 1, 1, 0), ("H", 4, 1, 1, 0), ("shift2", 0, 16), ("pad",),
    ("L", 4, 2, 0, 0), ("apply2", 8, 1), ("apply2", 4, 2), ("H", 4, 2, 0, 0),
    ("L", 4, 2, 1, 0), ("apply2", 0, 2), ("apply2", 7, 1), ("gH2",), ("apply2", 10, 1), ("H", 4, 2, 1, 0),
        ("apply2", 2, 1), ("egH2",),
    ("L", 4, 3, 0, 0), ("apply2", 6, 1), ("apply2", 15, 1), ("apply2", 9, 1), ("apply2", 3, 1), ("H", 4, 3, 0, 0),
    ("L", 4, 3, 1, 0), ("apply2", 11, 1), ("apply2", 12, 1), ("apply2", 13, 1), ("H", 4, 3, 1, 0),
        ("apply2", 14, 1), ("store", 0, 16),
]


def body(gcn, post, load=True):
    return [s for s in TURN if s[0] in LSTM_STAGES or (gcn if s[0] in GCN_STAGES else post)
            if load or s[0] != "loadx"]


PROLOGUE = [("loadx",), ("gZ",), ("egZ",), ("loadx",), ("gH1",), ("egH1",), ("level1",), ("gY",), ("egY",), ("gH2",),
            ("egH2",), ("pad",)]

EPILOGUE = [
    ("T", 0, 4), ("eT", 0, 4), ("T", 4, 4), ("stats1", 0, 4), ("T", 8, 4), ("var1", 0, 4), ("eT", 4, 4),
        ("eT", 8, 4), ("stats1", 4, 4), ("shift1", 0, 4), ("T", 12, 4), ("apply1", 1, 1), ("var1", 4, 4),
        ("applyd1", 0, 1), ("applyd1", 2, 1), ("applyd1", 3, 1), ("hi", 0, 4), ("shift1", 4, 4), ("lo", 0, 4),
        ("apply1", 5, 1), ("apply1", 4, 1), ("stats1", 8, 4), ("apply1", 6, 2), ("eT", 12, 4), ("var1", 8, 4),
        ("split", 4, 4), ("K", 0, 4), ("stats1", 14, 2), ("shift1", 8, 4), ("applyd1", 8, 1), ("applyd1", 9, 1),
        ("eK", 0, 4), ("apply1", 11, 1), ("apply1", 10, 1), ("stats1", 12, 2), ("K", 4, 4), ("eK", 4, 4),
        ("var1", 12, 4), ("shift1", 12, 4), ("split", 8, 4), ("O", 0, 4), ("bias", 0, 8), ("apply1", 12, 4),
        ("O", 4, 4), ("eO", 0, 4), ("K", 8, 4), ("hi", 12, 4), ("lo", 12, 4), ("eO", 4, 4), ("K", 12, 4),
        ("stats2", 0, 8), ("eK", 8, 4), ("var2", 0, 4), ("var2", 4, 4), ("eK", 12, 4), ("bias", 12, 4), ("O", 8, 4),
        ("bias", 8, 4), ("eO", 8, 4), ("stats2", 8, 4), ("shift2", 0, 4), ("shift2", 4, 4), ("var2", 8, 4),
        ("apply2", 4, 2), ("O", 12, 4), ("eO", 12, 4), ("apply2", 0, 4), ("stats2", 14, 2), ("shift2", 8, 4),
        ("apply2", 6, 2), ("stats2", 12, 2), ("apply2", 8, 4), ("var2", 12, 4), ("shift2", 12, 4), ("store", 0, 8),
        ("applyd2", 12, 4), ("store", 8, 4), ("store", 12, 4),
]

BANKS = {"gZ": 4, "gH1": 4, "gY": 4, "gH2": 4, "T": None, "K": 4, "O": None, "L": None}


def banks_of(stage):
    kind = stage[0]
    return BANKS[kind] or (len(gate_list(stage)) if kind == "L" else stage[2] * T // BANK)


def aligned(stage):
    return stage[0] != "L" and banks_of(stage) > 1



ADDS = {
    "loadx": {"xg_loaded0": 16, "xg_loaded1": 16},
    "loadr": {"xr_loaded": 16},
    "gZ": {"for_act": 2},
    "egZ": {"z_ready": 2},
    "gH1": {"for_dve": 2},
    "egH1": {"h1_ready": 2},
    "gY": {"for_dve": 2},
    "egY": {"y_ready": 2},
    "gH2": {"for_act": 2},
    "egH2": {"h2_hi_ready": 2, "h2_ready": 2},
    "T": {"for_dve": 1},
    "eT": {"u_ready": 1},
    "K": {"for_act": 1},
    "eK": {"zk_ready": 2},
    "O": {"for_dve": 1},
    "eO": {"v_ready": 1},
    "stats1": {"stats_ready": 1},
    "stats2": {"stats_ready": 1},
    "var1": {"var_ready": 1, "rstd_ready": 1, "dve_order": 5},
    "var2": {"var_ready": 1, "rstd_ready": 1, "dve_order": 5},
    "shift1": {"shift_ready": 1},
    "shift2": {"shift_ready": 1},
    "apply1": {"xn_ready": 1},
    "applyd1": {"xn_dve": 1},
    "apply2": {"out_ready": 1},
    "applyd2": {"out_dve": 1},
    "bias": {"r_ready": 1},
    "split": {"dve_order": 1, "parts_ready": 1},
    "hi": {"hi_ready": 1},
    "lo": {"parts_ready": 1},
    "store": {"stored": 16},
    "pad": {},
    "level1": {},
    "H": {"tanhc": 1, "h_done": 1, "dve_order": 2},
}
READ_BY = {"gZ": "z_ready", "gH1": "h1_ready", "gY": "y_ready", "gH2": "h2_ready", "T": "u_ready",
           "K": "zk_ready", "O": "v_ready", "L": "acts"}


DONE = {"eT": "u_ready", "shift1": "shift_ready", "apply1": "xn_ready", "applyd1": "xn_dve",
        "split": "parts_ready", "hi": "hi_ready", "lo": "parts_ready", "eK": "zk_ready", "bias": "r_ready",
        "eO": "v_ready", "shift2": "shift_ready", "apply2": "out_ready", "applyd2": "out_dve"}


def adds(stage):
    if stage[0] == "L":
        n = len(gate_list(stage))
        return {"gates": n, "acts": n, "c_ready": 1, "dve_order": 2 if stage[2] else 0}
    return ADDS[stage[0]]


NAMES = sorted({n for a in ADDS.values() for n in a} | set(adds(("L", 1, 1, 0, 0))))


class Segment:

    def __init__(self, stages, turns, chunk, before):
        self.stages, self.turns, self.chunk = stages, turns, chunk
        self.start = before.end() if before else dict.fromkeys(NAMES, 0)
        self.before = before
        self.through = []
        now = dict(self.start)
        for stage in stages:
            for name, n in adds(stage).items():
                now[name] += n
            self.through.append(dict(now))
        self.per_turn = {n: now[n] - self.start[n] for n in NAMES}
        self.banks, self.users = {}, [[] for _ in range(8)]
        at = 0
        for skip in range(8):
            at = 0
            for stage in stages:
                if stage[0] == "pad":
                    at += skip
                elif stage[0] in BANKS:
                    at += (aligned(stage) and at % 2) + banks_of(stage)
            if at % 8 == 0 or ("pad",) not in stages:
                break
        at = 0
        for k, stage in enumerate(stages):
            if stage[0] == "pad":
                at += skip
            if stage[0] not in BANKS:
                continue
            n = banks_of(stage)
            at += aligned(stage) and at % 2
            self.banks[k] = [(at + j) % 8 for j in range(n)]
            for j, bank in enumerate(self.banks[k]):
                self.users[bank].append((k, j))
            at += n

    def end(self):
        return {n: self.start[n] + self.turns * self.per_turn[n] for n in NAMES}

    def read(self, k, j):
        kind, *of = self.stages[k]
        name, by = READ_BY[kind], k if kind == "L" else self.stages.index(("e" + kind, *of))
        return name, self.through[by][name] - adds(self.stages[by])[name] + 1 + (j if kind == "L" else j // 2)

    def last_reads(self, bank):
        if not self.users[bank]:
            return {}
        name, at = self.read(*self.users[bank][-1])
        return {name: self.start[name] + self.per_turn[name] - at}

    def free(self, k, j):
        bank = self.banks[k][j]
        turn = self.users[bank].index((k, j))
        if turn:
            return [self.read(*self.users[bank][turn - 1])]
        waits = {}
        for seg in ([self.before] if self.before else []) + ([self] if self.turns > 1 else []):
            for name, short in seg.last_reads(bank).items():
                waits[name] = min(short, waits.get(name, short))
        return [(name, self.start[name] - short) for name, short in sorted(waits.items())]


def make_segments():
    segs = [Segment(PROLOGUE, 1, -1, None)]
    for stages, turns in ((body(True, False), 1), (body(True, True), CHUNKS - 3), (body(True, True, False), 1),
                          (body(False, True), 1), (EPILOGUE, 1)):
        chunk = sum(seg.turns for seg in segs) - 1
        segs.append(Segment(stages, turns, chunk, segs[-1]))
    return segs


def build(nc, x, adj_t, w_ih, w_hh, b_ih, b_hh, wg0, bg0, wg1, bg1, w_l1, b_l1, out):
    fp32, fp32r, fp16 = mybir.dt.float32, mybir.dt.float32r, mybir.dt.float16
    ALU, ACT = mybir.AluOpType, mybir.ActivationFunctionType
    segments = make_segments()
    ctx = ExitStack()
    with ctx:
        def sb(name, shape, dt=fp32):
            return ctx.enter_context(nc.sbuf_tensor(name, shape, dt))

        def sem(name):
            return ctx.enter_context(nc.semaphore(name))

        adj_sb = sb("adj_sb", [T, T])
        adj3 = sb("adj3", [T, 3, T])
        adj3_hi = sb("adj3_hi", [T, 3, T], fp32r)
        adj3_lo = sb("adj3_lo", [T, 3, T], fp32r)
        wg0_sb = sb("wg0_sb", [D, D])
        wg1_sb = sb("wg1_sb", [D, D])
        wl1_sb = sb("wl1_sb", [D, 3, D])
        wih_sb = sb("wih_sb", [D, LEVELS, 4, D])
        whh_sb = sb("whh_sb", [D, LEVELS - 1, 4, D])
        w1_hi = sb("w1_hi", [D, 4, D], fp32r)
        w1_lo = sb("w1_lo", [D, 4, D], fp32r)
        wih_hi = sb("wih_hi", [D, LEVELS - 1, 4, D], fp16)
        wih_lo = sb("wih_lo", [D, LEVELS - 1, 4, D], fp16)
        whh_hi = sb("whh_hi", [D, LEVELS - 1, 4, D], fp16)
        whh_lo = sb("whh_lo", [D, LEVELS - 1, 4, D], fp16)
        bih_sb = sb("bih_sb", [D, LEVELS, 4])
        bhh_sb = sb("bhh_sb", [D, LEVELS, 4])
        gate_bias = sb("gate_bias", [D, LEVELS, 4])
        bg0_rows = sb("bg0_rows", [T, D])
        bg1_rows = sb("bg1_rows", [T, D])
        bl1_rows = sb("bl1_rows", [T, D])
        bias1 = sb("bias1", [D, T])
        neg_bias1 = sb("neg_bias1", [D, T])
        bias2 = sb("bias2", [T, D])
        ident = sb("ident", [D, D], fp16)
        minus_half = sb("minus_half", [T, CB])
        xg = sb("xg", [T, CB, D])
        xr = sb("xr", [T, CB, D])
        z = sb("z", [D, CB, T])
        h1 = sb("h1", [D, CB, T])
        y = sb("y", [T, CB, D])
        h2_hi = sb("h2_hi", [D, CB, T], fp32r)
        h2_lo = sb("h2_lo", [D, CB, T], fp32r)
        h_hi = sb("h_hi", [D, CB, T], fp16)
        h_lo = sb("h_lo", [D, CB, T], fp16)
        u = sb("u", [T, CB, D])
        xn = sb("xn", [T, CB, D])
        xn_hi = sb("xn_hi", [T, CB, D], fp32r)
        xn_lo = sb("xn_lo", [T, CB, D], fp32r)
        zk = sb("zk", [D, CB, 3, T])
        v = sb("v", [T, CB, D])
        stats = sb("stats", [T, CB, 6])
        mean = sb("mean", [T, CB])
        diff = sb("diff", [T, CB])
        var = sb("var", [T, CB])
        rstd = [sb(f"rstd{norm}", [T, CB]) for norm in (1, 2)]
        shift = [sb(f"shift{norm}", [T, CB]) for norm in (1, 2)]
        gate = [[sb(f"gate{n}_{g}", [D, BANK]) for g in range(4)] for n in range(2)]
        tanh_c = [sb(f"tanh_c{n}", [D, BANK]) for n in range(2)]
        h_new = [sb(f"h_new{n}", [D, BANK]) for n in range(2)]
        cell = [sb(f"cell{a}", [D, BANK]) for a in range(STREAMS)]
        prev_hi = [sb(f"prev_hi{a}", [D, BANK], fp16) for a in range(STREAMS)]
        prev_lo = [sb(f"prev_lo{a}", [D, BANK], fp16) for a in range(STREAMS)]
        warm = prev_hi[0]
        ps = ctx.enter_context(nc.psum_tensor("ps", [128, 8, BANK], fp32))

        S = {name: sem(name) for name in NAMES}
        adj_loaded = sem("adj_loaded")
        bg0_loaded = sem("bg0_loaded")
        w_loaded = sem("w_loaded")
        level1_loaded = sem("level1_loaded")
        lstm_loaded = [sem(f"lstm_loaded{p}") for p in range(2, LEVELS + 1)]
        hi_made = sem("hi_made")
        lo_made = sem("lo_made")
        post_loaded = sem("post_loaded")
        masks_made = sem("masks_made")
        split_done = sem("split_done")
        warm_made = sem("warm_made")
        bias_ps = sem("bias_ps")
        bias_made = sem("bias_made")

        def value(seg, n, name, k=None):
            at = seg.start[name] if k is None else seg.through[k][name]
            return at if n is None else n * seg.per_turn[name] + at

        def made(seg, n, k, b0, nb, *kinds):
            found = {}
            for at, (kind, *of) in enumerate(seg.stages[:k]):
                if kind in kinds and of[0] < b0 + nb and b0 < of[0] + of[1]:
                    name = DONE[kind]
                    found[name] = value(seg, n, name, at)
            assert found
            return found.items()

        def sums(seg, k, nb):
            bank = seg.banks[k][0]
            return ps[:, bank:bank + nb * T // BANK, :].rearrange("t q (b d) -> t (q b) d", d=D)

        def pair(seg, k, half=0):
            bank = seg.banks[k][2 * half]
            return ps[:, bank:bank + 2, :].rearrange("d q (b t) -> d (q b) t", t=T)

        def walk(eng, run, segs):
            for seg in segs:
                if seg.turns == 1:
                    for k, stage in enumerate(seg.stages):
                        run(seg, None, k, stage)
                else:
                    with eng.Fori(0, seg.turns) as n:
                        for k, stage in enumerate(seg.stages):
                            run(seg, n, k, stage)

        SPLIT_AT = {("L", 1, 0, 1, 0): 2, ("L", 2, 0, 0, 0): 3, ("L", 3, 0, 0, 0): 4}

        def weight_parts(p):
            return [[t[:, p - 2 + off, :, :].rearrange("k g n -> k (g n)") for t, off in
                     ((w, w is wih_sb), (hi, 0), (lo, 0))]
                    for w, hi, lo in ((wih_sb, wih_hi, wih_lo), (whh_sb, whh_hi, whh_lo))]

        def lstm_index(seg, k):
            return sum(s[0] == seg.stages[k][0] for s in seg.stages[:k])

        def unit_done(seg, n, k, back):
            return value(seg, n, "h_done") + lstm_index(seg, k) + 1 - back

        def windows(stage):
            return SB * (T // stage[1]) if stage[1] > 1 else BANK

        def positions(arr, stage):
            _, p, s, stream, part = stage
            if p == 1:
                b0 = stream * SB + part * (BANK // T)
                return arr[:, b0:b0 + BANK // T, :]
            n = T // p
            part_of = arr[:, stream * SB:(stream + 1) * SB, 0:n * p]
            return part_of.rearrange("h b (w s) -> h b w s", s=p)[:, :, :, s]

        def shaped(ap, stage):
            return ap[:, 0:windows(stage)].rearrange("h (b w) -> h b w", w=T // stage[1])

        block = ctx.enter_context(nc.Block())

        @block.sync
        def _(sp):
            def run(seg, n, k, stage):
                chunk = seg.chunk if n is None else n + seg.chunk
                if stage == ("loadx",):
                    ahead = 1 if k == 0 else 2
                    if k:
                        sp.wait_ge(S["for_act"], value(seg, n, "for_act", seg.stages.index(("gZ",))))
                    for half in range(2):
                        sp.dma_start(xg[:, half * SB:(half + 1) * SB, :],
                                     x[:, bass.ds((chunk + ahead) * CB + half * SB, SB), :]
                                     ).then_inc(S[f"xg_loaded{half}"], 16)
                elif stage == ("loadr",):
                    if seg.chunk > 0:
                        sp.wait_ge(S["u_ready"], value(seg, n, "u_ready", k))
                    sp.dma_start(xr[:, :, :], x[:, bass.ds(chunk * CB, CB), :]).then_inc(S["xr_loaded"], 16)
                elif stage[0] == "store":
                    b0, nb = stage[1:]
                    for name, at in made(seg, n, k, b0, nb, "apply2", "applyd2"):
                        sp.wait_ge(S[name], at)
                    sp.dma_start(out[:, bass.ds((chunk - 1) * CB + b0, nb), :], v[:, b0:b0 + nb, :]
                                 ).then_inc(S["stored"], 16)

            sp.dma_start(adj_sb[:, :], adj_t).then_inc(adj_loaded, 16)
            sp.dma_start(bg0_rows[:, :], bg0).then_inc(bg0_loaded, 16)
            for half in range(2):
                sp.dma_start(xg[:, half * SB:(half + 1) * SB, :], x[:, half * SB:(half + 1) * SB, :]
                             ).then_inc(S[f"xg_loaded{half}"], 16)
                if half == 0:
                    for dst, src in ((wg0_sb[:, :], wg0), (wg1_sb[:, :], wg1), (bg1_rows[:, :], bg1)):
                        sp.dma_start(dst, src).then_inc(w_loaded, 16)
            for dst, src in ((wih_sb[:, 0, :, :], w_ih[:, 0, :, :]), (bih_sb[:, :, :], b_ih), (bhh_sb[:, :, :], b_hh)):
                sp.dma_start(dst, src).then_inc(level1_loaded, 16)
            for p in range(1, LEVELS):
                sp.dma_start(wih_sb[:, p, :, :], w_ih[:, p, :, :]).then_inc(lstm_loaded[p - 1], 16)
                sp.dma_start(whh_sb[:, p - 1, :, :], w_hh[:, p - 1, :, :]).then_inc(lstm_loaded[p - 1], 16)
            run(segments[0], None, 3, segments[0].stages[3])
            for dst, src in ((wl1_sb[:, :, :], w_l1), (bl1_rows[:, :], b_l1)):
                sp.dma_start(dst, src).then_inc(post_loaded, 16)
            walk(sp, run, segments[1:])
            sp.wait_ge(S["stored"], segments[-1].end()["stored"])

        W_LOADS, LEVEL1_LOADS, LEVEL_LOADS, POST_LOADS = 3 * 16, 3 * 16, 2 * 16, 2 * 16

        @block.gpsimd
        def _(pool):
            nc.gpsimd.memset(ident[:, :], 0.0).then_inc(masks_made, 1)
            nc.gpsimd.memset(minus_half[:, :], -0.5).then_inc(masks_made, 1)
            pool.wait_ge(masks_made, 1)
            nc.gpsimd.affine_select(out=ident[:, :], in_=ident[:, :], compare_op=ALU.not_equal, fill=1.0,
                                    base=0, pattern=[[-1, D]], channel_multiplier=1).then_inc(masks_made, 1)
            pool.wait_ge(adj_loaded, 16)
            for part, (op, sign) in enumerate(((ALU.is_equal, 1), (ALU.is_gt, 1), (ALU.is_gt, -1))):
                nc.gpsimd.affine_select(out=adj3[:, part, :], in_=adj_sb[:, :], compare_op=op, fill=0.0,
                                        base=0, pattern=[[-sign, T]],
                                        channel_multiplier=sign).then_inc(masks_made, 1)

            def run(seg, n, k, stage):
                if stage[0] in ("var1", "var2"):
                    pool.wait_ge(S["var_ready"], value(seg, n, "var_ready", k))
                    some = slice(stage[1], stage[1] + stage[2])
                    nc.gpsimd.tensor_tensor(out=rstd[int(stage[0][-1]) - 1][:, some], in0=var[:, some],
                                            in1=minus_half[:, some],
                                            op=ALU.pow).then_inc(S["rstd_ready"], 1)

            pool.wait_ge(masks_made, 6)
            walk(pool, run, segments)

        @block.scalar
        def _(act):
            def run(seg, n, k, stage):
                kind = stage[0]
                if seg is segments[1] and stage in SPLIT_AT:
                    act.wait_ge(lstm_loaded[SPLIT_AT[stage] - 2], LEVEL_LOADS)
                    for w, hi, lo in weight_parts(SPLIT_AT[stage]):
                        nc.scalar.activation(hi, w, ACT.Copy, scale=WSCALE).then_inc(hi_made, 1)
                if kind in ("egZ", "egH2"):
                    made_by = seg.stages.index((kind[1:],))
                    for half in range(2):
                        act.wait_ge(S["for_act"], value(seg, n, "for_act", made_by) - 1 + half)
                        some = slice(half * SB, (half + 1) * SB)
                        if kind == "egZ":
                            nc.scalar.activation(z[:, some, :], pair(seg, made_by, half),
                                                 ACT.Copy).then_inc(S["z_ready"], 1)
                        else:
                            nc.scalar.activation(h2_hi[:, some, :], pair(seg, made_by, half),
                                                 ACT.Relu).then_inc(S["h2_hi_ready"], 1)
                elif kind == "eK":
                    made_by = seg.stages.index(("K", *stage[1:]))
                    act.wait_ge(S["for_act"], value(seg, n, "for_act", made_by))
                    for half in range(2):
                        b0, bank = stage[1] + 2 * half, seg.banks[made_by][2 * half]
                        nc.scalar.activation(zk[:, b0:b0 + 2, :, :].rearrange("d b k t -> d b (k t)"),
                                             ps[:, bank:bank + 2, 0:3 * T], ACT.Copy).then_inc(S["zk_ready"], 1)
                elif kind == "L":
                    _, p, s, stream, part = stage
                    unit, w = lstm_index(seg, k) % 2, windows(stage)
                    gates = gate_list(stage)
                    if not (seg.start["h_done"] == 0 and lstm_index(seg, k) < 2):
                        act.wait_ge(S["h_done"], unit_done(seg, n, k, 2))
                    ready = value(seg, n, "gates", k)
                    for j, g in enumerate(gates):
                        act.wait_ge(S["gates"], ready - len(gates) + 1 + j)
                        nc.scalar.activation(gate[unit][g][:, 0:w], ps[:, seg.banks[k][j], 0:w],
                                             ACT.Tanh if g == GG else ACT.Sigmoid,
                                             bias=gate_bias[:, p - 1, g:g + 1],
                                             scale=1.0 if p == 1 else 1.0 / WSCALE).then_inc(S["acts"], 1)
                elif kind == "H":
                    unit, w = lstm_index(seg, k) % 2, windows(stage)
                    act.wait_ge(S["c_ready"], value(seg, n, "c_ready", k))
                    nc.scalar.activation(tanh_c[unit][:, 0:w], cell[unit][:, 0:w],
                                         ACT.Tanh).then_inc(S["tanhc"], 1)
                elif kind in ("apply1", "apply2"):
                    src, dst, name = (u, xn, "xn_ready") if kind == "apply1" else (v, v, "out_ready")
                    b0, nb = stage[1:]
                    norm = int(kind[-1]) - 1
                    for other, at in made(seg, n, k, b0, nb, f"shift{norm + 1}"):
                        act.wait_ge(S[other], at)
                    for b in range(b0, b0 + nb):
                        last = nc.scalar.activation(dst[:, b, :], src[:, b, :], ACT.Identity,
                                                    bias=shift[norm][:, b:b + 1],
                                                    scale=rstd[norm][:, b:b + 1])
                    last.then_inc(S[name], 1)

                elif kind == "hi":
                    b0, nb = stage[1:]
                    for other, at in made(seg, n, k, b0, nb, "apply1", "applyd1"):
                        act.wait_ge(S[other], at)
                    nc.scalar.activation(xn_hi[:, b0:b0 + nb, :], xn[:, b0:b0 + nb, :],
                                         ACT.Copy).then_inc(S["hi_ready"], 1)

            walk(act, run, segments[:1])
            act.wait_ge(split_done, 1)
            walk(act, run, segments[1:])

        @block.vector
        def _(dve):
            nc.vector.memset(warm[:, :], 0.0).then_inc(warm_made, 1)
            dve.wait_ge(bias_ps, 1)
            nc.vector.tensor_copy(bias1[:, :], ps[:, 6, 0:T]).then_inc(bias_made, 1)
            nc.vector.tensor_scalar(neg_bias1[:, :], ps[:, 6, 0:T], -1.0, None, ALU.mult).then_inc(bias_made, 1)
            dve.wait_ge(bias_ps, 2)
            dve.wait_ge(w_loaded, W_LOADS)
            nc.vector.tensor_tensor(out=bias2[:, :], in0=ps[:, 7, 0:D], in1=bg1_rows[:, :],
                                    op=ALU.add).then_inc(bias_made, 1)
            def split(src, hi, lo, count):
                nc.vector.tensor_copy(hi, src).then_inc(split_done, 1)
                dve.wait_ge(split_done, count)
                nc.vector.tensor_tensor(out=lo, in0=src, in1=hi.bitcast(fp32), op=ALU.subtract).then_inc(split_done, 1)

            def low_weights(p):
                dve.wait_ge(hi_made, 2 * (p - 1))
                for w, hi, lo in weight_parts(p):
                    nc.vector.scalar_tensor_tensor(out=lo, in0=w, scalar=WSCALE, in1=hi, op0=ALU.mult,
                                                   op1=ALU.subtract).then_inc(lo_made, 1)

            def variances(seg, n, k, b0, nb):
                base = value(seg, n, "dve_order", k) - 5
                count = [0]

                def link(ins, wait=True):
                    count[0] += 1
                    ins.then_inc(S["dve_order"], 1)
                    if wait:
                        dve.wait_ge(S["dve_order"], base + count[0])

                dve.wait_ge(S["stats_ready"], value(seg, n, "stats_ready", k))
                even, odd, in_even, in_odd = (stats[:, b0:b0 + nb, field] for field in (1, 4, 2, 5))
                d, m, q = (t[:, b0:b0 + nb] for t in (diff, mean, var))
                link(nc.vector.tensor_tensor(out=d, in0=even, in1=odd, op=ALU.subtract), False)
                link(nc.vector.tensor_tensor(out=m, in0=even, in1=odd, op=ALU.add), False)
                link(nc.vector.tensor_tensor(out=q, in0=in_even, in1=in_odd, op=ALU.add))
                link(nc.vector.tensor_tensor(out=d, in0=d, in1=d, op=ALU.mult), False)
                link(nc.vector.tensor_scalar(q, q, 1.0 / D, EPS, ALU.mult, ALU.add))
                nc.vector.scalar_tensor_tensor(out=q, in0=d, scalar=0.25, in1=q,
                                               op0=ALU.mult, op1=ALU.add).then_inc(S["var_ready"], 1)

            def run(seg, n, k, stage):
                kind = stage[0]
                if seg is segments[1] and stage in SPLIT_AT:
                    low_weights(SPLIT_AT[stage])
                if seg is segments[1] and stage == ("L", 4, 0, 0, 0):
                    dve.wait_ge(masks_made, 6)
                    flat = "s k t -> s (k t)"
                    split(adj3[:, :, :].rearrange(flat), adj3_hi[:, :, :].rearrange(flat),
                          adj3_lo[:, :, :].rearrange(flat), 4)
                    dve.wait_ge(post_loaded, POST_LOADS)
                if kind == "level1":
                    dve.wait_ge(level1_loaded, LEVEL1_LOADS)
                    nc.vector.tensor_tensor(out=gate_bias[:, :, :], in0=bih_sb[:, :, :], in1=bhh_sb[:, :, :],
                                            op=ALU.add).then_inc(split_done, 1)
                    split(wih_sb[:, 0, :, :].rearrange("k g n -> k (g n)"), w1_hi[:, :, :].rearrange("k g n -> k (g n)"),
                          w1_lo[:, :, :].rearrange("k g n -> k (g n)"), 2)
                if kind == "egY" and seg is segments[0]:
                    dve.wait_ge(bias_made, 3)
                if kind in ("egH1", "egY", "egH2", "eT", "eO"):
                    made_by = seg.stages.index((kind[1:], *stage[1:]))
                    products = value(seg, n, "for_dve", made_by)
                if kind in ("egH1", "egY"):
                    dst, tile, op, name = ((h1, neg_bias1, ALU.max, "h1_ready") if kind == "egH1" else
                                           (y, bias2, ALU.add, "y_ready"))
                    for half in range(2):
                        dve.wait_ge(S["for_dve"], products - 1 + half)
                        nc.vector.tensor_tensor(out=dst[:, half * SB:(half + 1) * SB, :],
                                                in0=pair(seg, made_by, half),
                                                in1=tile[:, :].unsqueeze(1).broadcast_to([128, SB, 128]),
                                                op=op).then_inc(S[name], 1)
                elif kind == "egH2":
                    for half in range(2):
                        dve.wait_ge(S["h2_hi_ready"], value(seg, n, "h2_hi_ready", k) - 1 + half)
                        some = slice(half * SB, (half + 1) * SB)
                        nc.vector.scalar_tensor_tensor(out=h2_lo[:, some, :], in0=pair(seg, made_by, half), scalar=0.0,
                                                       in1=h2_hi[:, some, :].bitcast(fp32), op0=ALU.max,
                                                       op1=ALU.subtract).then_inc(S["h2_ready"], 1)
                elif kind == "eT":
                    b0, nb = stage[1:]
                    dve.wait_ge(S["for_dve"], products)
                    dve.wait_ge(S["xr_loaded"], value(seg, n, "xr_loaded"))
                    nc.vector.tensor_tensor(out=u[:, b0:b0 + nb, :], in0=sums(seg, made_by, nb),
                                            in1=xr[:, b0:b0 + nb, :], op=ALU.add).then_inc(S["u_ready"], 1)
                elif kind == "eO":
                    b0, nb = stage[1:]
                    dve.wait_ge(S["for_dve"], products)
                    for name, at in made(seg, n, k, b0, nb, "bias"):
                        dve.wait_ge(S[name], at)
                    if seg.start["out_ready"] or n is not None:
                        dve.wait_ge(S["stored"], value(seg, n, "stored"))
                    nc.vector.tensor_tensor(out=v[:, b0:b0 + nb, :], in0=sums(seg, made_by, nb),
                                            in1=xn[:, b0:b0 + nb, :], op=ALU.add).then_inc(S["v_ready"], 1)
                elif kind in ("stats1", "stats2"):
                    b0, nb = stage[1:]
                    for name, at in made(seg, n, k, b0, nb, "eT" if kind == "stats1" else "eO"):
                        dve.wait_ge(S[name], at)
                    for b in range(b0, b0 + nb):
                        last = nc.vector.bn_stats(stats[:, b, :], (u if kind == "stats1" else v)[:, b, :])
                    last.then_inc(S["stats_ready"], 1)
                elif kind in ("var1", "var2"):
                    variances(seg, n, k, *stage[1:])
                elif kind in ("shift1", "shift2"):
                    norm, some = int(kind[-1]) - 1, slice(stage[1], stage[1] + stage[2])
                    at = max(j for j in range(k) if seg.stages[j][0] == f"var{norm + 1}"
                             and seg.stages[j][1:] == stage[1:])
                    dve.wait_ge(S["rstd_ready"], value(seg, n, "rstd_ready", at))
                    nc.vector.scalar_tensor_tensor(out=shift[norm][:, some], in0=mean[:, some], scalar=-0.5,
                                                   in1=rstd[norm][:, some],
                                                   op0=ALU.mult, op1=ALU.mult).then_inc(S["shift_ready"], 1)
                elif kind in ("applyd1", "applyd2"):
                    b0, nb = stage[1:]
                    norm = int(kind[-1]) - 1
                    src, dst = ((u, xn), (v, v))[norm]
                    for name, at in made(seg, n, k, b0, nb, f"shift{norm + 1}"):
                        dve.wait_ge(S[name], at)
                    for b in range(b0, b0 + nb):
                        last = nc.vector.tensor_scalar(dst[:, b, :], src[:, b, :], rstd[norm][:, b:b + 1],
                                                       shift[norm][:, b:b + 1], ALU.mult, ALU.add)
                    last.then_inc(S[DONE[kind]], 1)
                elif kind == "split":
                    b0, nb = stage[1:]
                    for name, at in made(seg, n, k, b0, nb, "apply1", "applyd1"):
                        dve.wait_ge(S[name], at)
                    some = slice(b0, b0 + nb)
                    nc.vector.tensor_copy(xn_hi[:, some, :], xn[:, some, :]).then_inc(S["dve_order"], 1)
                    dve.wait_ge(S["dve_order"], value(seg, n, "dve_order", k))
                    nc.vector.tensor_tensor(out=xn_lo[:, some, :], in0=xn[:, some, :],
                                            in1=xn_hi[:, some, :].bitcast(fp32),
                                            op=ALU.subtract).then_inc(S["parts_ready"], 1)
                elif kind == "lo":
                    b0, nb = stage[1:]
                    for name, at in made(seg, n, k, b0, nb, "hi"):
                        dve.wait_ge(S[name], at)
                    some = slice(b0, b0 + nb)
                    nc.vector.tensor_tensor(out=xn_lo[:, some, :], in0=xn[:, some, :],
                                            in1=xn_hi[:, some, :].bitcast(fp32),
                                            op=ALU.subtract).then_inc(S["parts_ready"], 1)
                elif kind == "bias":
                    b0, nb = stage[1:]
                    for name, at in made(seg, n, k, b0, nb, "split", "lo"):
                        dve.wait_ge(S[name], at)
                    nc.vector.tensor_tensor(out=xn[:, b0:b0 + nb, :], in0=xn[:, b0:b0 + nb, :],
                                            in1=bl1_rows[:, :].unsqueeze(1).broadcast_to([T, nb, D]),
                                            op=ALU.add).then_inc(S["r_ready"], 1)
                elif kind == "L":
                    unit, w = lstm_index(seg, k) % 2, windows(stage)
                    c, (cand, i_gate, f_gate) = cell[unit][:, 0:w], (gate[unit][g][:, 0:w] for g in (GG, GI, GF))
                    acts = value(seg, n, "acts", k)
                    dve.wait_ge(S["acts"], acts - len(gate_list(stage)) + 2)
                    if stage[2] == 0:
                        nc.vector.tensor_tensor(out=c, in0=i_gate, in1=cand, op=ALU.mult).then_inc(S["c_ready"], 1)
                    else:
                        nc.vector.tensor_tensor(out=cand, in0=i_gate, in1=cand,
                                                op=ALU.mult).then_inc(S["dve_order"], 1)
                        dve.wait_ge(S["acts"], acts - 1)
                        nc.vector.tensor_tensor(out=c, in0=f_gate, in1=c, op=ALU.mult).then_inc(S["dve_order"], 1)
                        dve.wait_ge(S["dve_order"], value(seg, n, "dve_order", k))
                        nc.vector.tensor_tensor(out=c, in0=c, in1=cand, op=ALU.add).then_inc(S["c_ready"], 1)
                elif kind == "H":
                    _, p, s, stream, _ = stage
                    unit, w = lstm_index(seg, k) % 2, windows(stage)
                    order = value(seg, n, "dve_order", k)
                    if s == p - 1:
                        hi, lo = positions(h_hi, stage), positions(h_lo, stage)
                    else:
                        hi, lo = shaped(prev_hi[stream], stage), shaped(prev_lo[stream], stage)
                    dve.wait_ge(S["acts"], value(seg, n, "acts", seg.stages.index(("L", *stage[1:]))))
                    dve.wait_ge(S["tanhc"], value(seg, n, "tanhc", k))
                    nc.vector.tensor_tensor(out=h_new[unit][:, 0:w], in0=gate[unit][GO][:, 0:w],
                                            in1=tanh_c[unit][:, 0:w], op=ALU.mult).then_inc(S["dve_order"], 1)
                    dve.wait_ge(S["dve_order"], order - 1)
                    if p == 1 and ("T", stream * SB, SB) in seg.stages:
                        dve.wait_ge(S["for_dve"], value(seg, n, "for_dve", seg.stages.index(("T", stream * SB, SB))))
                    h = shaped(h_new[unit], stage)
                    nc.vector.tensor_copy(hi, h).then_inc(S["dve_order"], 1)
                    dve.wait_ge(S["dve_order"], order)
                    nc.vector.tensor_tensor(out=lo, in0=h, in1=hi, op=ALU.subtract).then_inc(S["h_done"], 1)

            walk(dve, run, segments)

        @block.tensor
        def _(pe):
            pe.wait_ge(warm_made, 1)
            for _ in range(WARM_UP):
                nc.tensor.matmul(ps[:, 5, :], warm[:, 0:128], warm[:, :], start=True, stop=True)
            pe.wait_ge(adj_loaded, 16)
            pe.wait_ge(bg0_loaded, 16)
            nc.tensor.matmul(ps[:, 6, 0:T], bg0_rows[:, :], adj_sb[:, :], start=True, stop=True).then_inc(bias_ps, 1)

            def free(seg, n, k, j, count=1):
                waits = {}
                for jj in range(j, j + count):
                    for name, at in seg.free(k, jj):
                        waits[name] = max(at, waits.get(name, at))
                for name, at in waits.items():
                    pe.wait_ge(S[name], at if n is None else n * seg.per_turn[name] + at)

            def run(seg, n, k, stage):
                kind = stage[0]
                if kind not in BANKS:
                    return
                if seg is segments[1] and kind == "L" and stage[1] > 1 and stage[2:4] == (0, 0):
                    pe.wait_ge(lo_made, 2 * (stage[1] - 1))
                if seg is segments[2] and k == 0:
                    pe.wait_ge(post_loaded, POST_LOADS)
                    pe.wait_ge(split_done, 5)
                    pe.wait_ge(masks_made, 3)
                if kind == "gZ":
                    for half in range(2):
                        if seg is segments[0] and half == 1:
                            pe.wait_ge(w_loaded, W_LOADS)
                            pe.wait_ge(bias_made, 2)
                            nc.tensor.matmul(ps[:, 7, 0:D], bias1[:, :], wg1_sb[:, :], start=True,
                                             stop=True).then_inc(bias_ps, 1)
                        name = f"xg_loaded{half}"
                        pe.wait_ge(S[name], value(seg, n, name, k))
                        free(seg, n, k, 2 * half, 2)
                        for j in range(SB):
                            last = nc.tensor.matmul(pair(seg, k, half)[:, j, :], xg[:, half * SB + j, :],
                                                    adj_sb[:, :], start=True, stop=True)
                        last.then_inc(S["for_act"], 1)
                elif kind == "gH1":
                    if seg is segments[0]:
                        pe.wait_ge(bias_made, 3)
                    for half in range(2):
                        free(seg, n, k, 2 * half, 2)
                        pe.wait_ge(S["z_ready"], value(seg, n, "z_ready", seg.stages.index(("egZ",))) - 1 + half)
                        for q in (2 * half, 2 * half + 1):
                            last = nc.tensor.matmul(ps[:, seg.banks[k][q], :], wg0_sb[:, :], z[:, 4 * q:4 * q + 4, :],
                                                    start=True, stop=True)
                        last.then_inc(S["for_dve"], 1)
                elif kind == "gY":
                    for half in range(2):
                        free(seg, n, k, 2 * half, 2)
                        pe.wait_ge(S["h1_ready"], value(seg, n, "h1_ready", seg.stages.index(("egH1",))) - 1 + half)
                        for j in range(SB):
                            last = nc.tensor.matmul(pair(seg, k, half)[:, j, :], h1[:, half * SB + j, :],
                                                    wg1_sb[:, :], start=True, stop=True)
                        last.then_inc(S["for_dve"], 1)
                elif kind == "gH2":
                    for half in range(2):
                        free(seg, n, k, 2 * half, 2)
                        pe.wait_ge(S["y_ready"], value(seg, n, "y_ready", seg.stages.index(("egY",))) - 1 + half)
                        for j in range(SB):
                            last = nc.tensor.matmul(pair(seg, k, half)[:, j, :], y[:, half * SB + j, :],
                                                    adj_sb[:, :], start=True, stop=True)
                        last.then_inc(S["for_act"], 1)
                elif kind == "T":
                    b0, nb = stage[1:]
                    free(seg, n, k, 0, len(seg.banks[k]))
                    pe.wait_ge(S["h_done"], value(seg, n, "h_done") - (1 if b0 + nb <= SB else 0))
                    for j in range(nb):
                        o = sums(seg, k, nb)[:, j, :]
                        nc.tensor.matmul(o, h_hi[:, b0 + j, :], ident[:, :], start=True, stop=False)
                        last = nc.tensor.matmul(o, h_lo[:, b0 + j, :], ident[:, :], start=False, stop=True)
                    last.then_inc(S["for_dve"], 1)
                elif kind == "K":
                    b0, nb = stage[1:]
                    for name, at in made(seg, n, k, b0, nb, "split", "lo"):
                        pe.wait_ge(S[name], at)
                    a_hi, a_lo = (t[:, :, :].rearrange("s k t -> s (k t)") for t in (adj3_hi, adj3_lo))
                    for j in range(nb):
                        free(seg, n, k, j)
                        o = ps[:, seg.banks[k][j], 0:3 * T]
                        nc.tensor.matmul(o, xn_hi[:, b0 + j, :], a_hi, start=True, stop=False)
                        nc.tensor.matmul(o, xn_hi[:, b0 + j, :], a_lo, start=False, stop=False)
                        last = nc.tensor.matmul(o, xn_lo[:, b0 + j, :], a_hi, start=False, stop=True)
                    last.then_inc(S["for_act"], 1)
                elif kind == "O":
                    b0, nb = stage[1:]
                    free(seg, n, k, 0, len(seg.banks[k]))
                    for name, at in made(seg, n, k, b0, nb, "eK"):
                        pe.wait_ge(S[name], at)
                    for j in range(nb):
                        for part in range(3):
                            last = nc.tensor.matmul(sums(seg, k, nb)[:, j, :], zk[:, b0 + j, part, :],
                                                    wl1_sb[:, part, :], start=part == 0, stop=part == 2)
                    last.then_inc(S["for_dve"], 1)
                elif kind == "L":
                    _, p, s, stream, part = stage
                    gates = gate_list(stage)
                    if p == 1:
                        pe.wait_ge(S["h2_ready"], value(seg, n, "h2_ready") - 1 + stream)
                        for j, g in enumerate(gates):
                            free(seg, n, k, j)
                            o = ps[:, seg.banks[k][j], :]
                            x_hi, x_lo = positions(h2_hi, stage), positions(h2_lo, stage)
                            nc.tensor.matmul(o, w1_hi[:, g, :], x_hi, start=True, stop=False)
                            nc.tensor.matmul(o, w1_hi[:, g, :], x_lo, start=False, stop=False)
                            nc.tensor.matmul(o, w1_lo[:, g, :], x_hi, start=False,
                                             stop=True).then_inc(S["gates"], 1)
                        return
                    if s == 0:
                        pe.wait_ge(S["h_done"], unit_done(seg, n, k, 3 if p == 2 and stream == 0 else 2))
                    x_hi, x_lo = positions(h_hi, stage), positions(h_lo, stage)
                    w_hi, w_lo = wih_hi[:, p - 2, :, :], wih_lo[:, p - 2, :, :]
                    for j, g in enumerate(gates):
                        free(seg, n, k, j)
                        o = shaped(ps[:, seg.banks[k][j], :], stage)
                        nc.tensor.matmul(o, w_hi[:, g, :], x_hi, start=True, stop=False)
                        nc.tensor.matmul(o, w_hi[:, g, :], x_lo, start=False, stop=False)
                        last = nc.tensor.matmul(o, w_lo[:, g, :], x_hi, start=False, stop=s == 0)
                        if s == 0:
                            last.then_inc(S["gates"], 1)
                    if s > 0:
                        pe.wait_ge(S["h_done"], unit_done(seg, n, k, 2))
                        x_hi, x_lo = shaped(prev_hi[stream], stage), shaped(prev_lo[stream], stage)
                        w_hi, w_lo = whh_hi[:, p - 2, :, :], whh_lo[:, p - 2, :, :]
                        for j, g in enumerate(gates):
                            o = shaped(ps[:, seg.banks[k][j], :], stage)
                            nc.tensor.matmul(o, w_hi[:, g, :], x_hi, start=False, stop=False)
                            nc.tensor.matmul(o, w_hi[:, g, :], x_lo, start=False, stop=False)
                            nc.tensor.matmul(o, w_lo[:, g, :], x_hi, start=False,
                                             stop=True).then_inc(S["gates"], 1)

            walk(pe, run, segments[:1])
            pe.wait_ge(split_done, 3)
            walk(pe, run, segments[1:])


def kernel(**inputs):
    import numpy as np
    import concourse.bacc as bacc
    from concourse.bass_utils import run_bass_kernel_spmd

    def f(a):
        return np.asarray(a)

    ih, hh = f(inputs["L0_gnn_Wih"]), f(inputs["L0_gnn_Whh"])
    rows = lambda a: np.broadcast_to(f(a)[None, :], (T, D))
    arrays = {
        "x": f(inputs["x"]).transpose(1, 0, 2),
        "adj_t": f(inputs["adj"]).T,
        "w_ih": ih.reshape(LEVELS, 4, D, D).transpose(3, 0, 1, 2),
        "w_hh": hh.reshape(LEVELS, 4, D, D)[1:].transpose(3, 0, 1, 2),
        "b_ih": f(inputs["L0_gnn_bih"]).reshape(LEVELS, 4, D).transpose(2, 0, 1),
        "b_hh": f(inputs["L0_gnn_bhh"]).reshape(LEVELS, 4, D).transpose(2, 0, 1),
        "wg0": f(inputs["L0_gnn_Wg0"]),
        "bg0": rows(inputs["L0_gnn_bg0"]),
        "wg1": f(inputs["L0_gnn_Wg1"]),
        "bg1": rows(inputs["L0_gnn_bg1"]),
        "w_l1": f(inputs["L1_gnn_W"]).transpose(1, 0, 2),
        "b_l1": rows(inputs["L1_gnn_bias"]),
    }
    nc = bacc.Bacc("TRN2", target_bir_lowering=False, num_devices=1)
    feeds, aps = {}, []
    for name, a in arrays.items():
        feeds[name] = np.ascontiguousarray(a)
        aps.append(nc.dram_tensor(name, a.shape, mybir.dt.float32, kind="ExternalInput").ap())
    out = nc.dram_tensor("out", (T, B, D), mybir.dt.float32, kind="ExternalOutput").ap()
    build(nc, *aps, out)
    got = run_bass_kernel_spmd(nc, [feeds], core_ids=[0]).results[0]["out"]
    return got.transpose(1, 0, 2)
```
